# Optimizing a Trainium2 kernel written in Bass

```python
import numpy as np
import jax
import jax.numpy as jnp

def _softmax(x, axis=-1):
    return jax.nn.softmax(x, axis=axis)

def _gelu(x):
    return jax.nn.gelu(x, approximate=True)

def _silu(x):
    return jax.nn.silu(x)

def _sigmoid(x):
    return jax.nn.sigmoid(x)

def _layernorm(x, axis=-1, eps=1e-05):
    m = jnp.mean(x, axis=axis, keepdims=True)
    v = jnp.var(x, axis=axis, keepdims=True)
    return (x - m) / jnp.sqrt(v + eps)

def _scatter_add(tgt, idx, src, axis=0):
    return tgt.at[idx].add(src)

def _segment_sum(src, seg, n):
    return jax.ops.segment_sum(src, seg, n)
kernel_name = 'mk_seq_postln_d1_jaxref_r8_d1ba2f'

def setup_inputs(seed: int=0):
    np.random.seed(seed)
    _w = jnp.asarray

    def _L0_attn_setup():
        import jax, jax.numpy as jnp
        import numpy as np
        HIDDEN = 512
        NUM_HEADS = 32
        HEAD_DIM = HIDDEN // NUM_HEADS

        def _fp8_roundtrip(x):
            return x.astype(jnp.float8_e4m3fn).astype(jnp.float32)
        key = jax.random.key(seed)
        ks = jax.random.split(key, 10)
        B, S = (2, 512)
        hidden_states = jax.random.normal(ks[0], (B, S, HIDDEN), dtype=jnp.float32)
        scale = 0.02

        def lin(kw, kb):
            w = jax.random.normal(kw, (HIDDEN, HIDDEN), dtype=jnp.float32) * scale
            b = jax.random.normal(kb, (HIDDEN,), dtype=jnp.float32) * scale
            return (w, b)
        wq, bq = lin(ks[1], ks[2])
        wk, bk = lin(ks[3], ks[4])
        wv, bv = lin(ks[5], ks[6])
        wl, bl = lin(ks[7], ks[8])
        wq, bq = (_fp8_roundtrip(wq), _fp8_roundtrip(bq))
        wk, bk = (_fp8_roundtrip(wk), _fp8_roundtrip(bk))
        wv, bv = (_fp8_roundtrip(wv), _fp8_roundtrip(bv))
        return {'hidden_states': hidden_states, 'wq': wq, 'bq': bq, 'wk': wk, 'bk': bk, 'wv': wv, 'bv': bv, 'wl': wl, 'bl': bl}
    _L0_attn_in = _L0_attn_setup()

    def _L0_ffn_setup():
        import jax, jax.numpy as jnp
        import numpy as np
        import math
        B, S, IN, OUT = (4, 256, 512, 512)
        E, R, K = (8, 64, 128)
        SCALE = 64.0 / 64.0
        MULTIPLIER = 1.0
        key = jax.random.key(seed)
        ks = jax.random.split(key, 6)
        return {'x': jax.random.normal(ks[0], (B, S, IN), jnp.float32), 'W_org': jax.random.normal(ks[1], (OUT, IN), jnp.float32) * 0.02, 'lora_down': jax.random.normal(ks[2], (E, IN, R), jnp.float32) * 0.02, 'lora_up': jax.random.normal(ks[3], (E, R, OUT), jnp.float32) * 0.02, 'lora_keys': jax.random.normal(ks[4], (E, K), jnp.float32), 'Wq': jax.random.normal(ks[5], (K, IN), jnp.float32) * 0.02}
    _L0_ffn_in = _L0_ffn_setup()
    _d = {'L0_attn_hidden_states': _L0_attn_in['hidden_states'], 'L0_attn_wq': _L0_attn_in['wq'], 'L0_attn_bq': _L0_attn_in['bq'], 'L0_attn_wk': _L0_attn_in['wk'], 'L0_attn_bk': _L0_attn_in['bk'], 'L0_attn_wv': _L0_attn_in['wv'], 'L0_attn_bv': _L0_attn_in['bv'], 'L0_attn_wl': _L0_attn_in['wl'], 'L0_attn_bl': _L0_attn_in['bl'], 'L0_ffn_W_org': _L0_ffn_in['W_org'], 'L0_ffn_lora_down': _L0_ffn_in['lora_down'], 'L0_ffn_lora_up': _L0_ffn_in['lora_up'], 'L0_ffn_lora_keys': _L0_ffn_in['lora_keys'], 'L0_ffn_Wq': _L0_ffn_in['Wq']}
    _x0 = _d['L0_attn_hidden_states']
    _d['L0_attn_hidden_states'] = jax.random.normal(jax.random.fold_in(jax.random.key(seed), 1), (4, 256, 512), dtype=_x0.dtype)
    del _x0
    return _d

def reference(L0_attn_hidden_states, L0_attn_wq, L0_attn_bq, L0_attn_wk, L0_attn_bk, L0_attn_wv, L0_attn_bv, L0_attn_wl, L0_attn_bl, L0_ffn_W_org, L0_ffn_lora_down, L0_ffn_lora_up, L0_ffn_lora_keys, L0_ffn_Wq):

    def _L0_attn_ref(hidden_states, wq, bq, wk, bk, wv, bv, wl, bl):
        import jax, jax.numpy as jnp
        import numpy as np
        HIDDEN = 512
        NUM_HEADS = 32
        HEAD_DIM = HIDDEN // NUM_HEADS

        def _fp8_roundtrip(x):
            return x.astype(jnp.float8_e4m3fn).astype(jnp.float32)
        B, S, E = hidden_states.shape
        H, D = (NUM_HEADS, HEAD_DIM)
        q = (hidden_states @ wq.T + bq).reshape(B, S, H, D)
        k = (hidden_states @ wk.T + bk).reshape(B, S, H, D)
        v = (hidden_states @ wv.T + bv).reshape(B, S, H, D)
        latent = hidden_states @ wl.T + bl
        scores = jnp.einsum('bshd,bstd->bsht', q, k) / np.sqrt(D).astype(np.float32)
        probs = jax.nn.softmax(scores, axis=-1)
        context = jnp.einsum('bsht,bstd->bshd', probs, v).reshape(B, S, E)
        return context

    def _L0_ffn_ref(x, W_org, lora_down, lora_up, lora_keys, Wq):
        import jax, jax.numpy as jnp
        import numpy as np
        import math
        B, S, IN, OUT = (4, 256, 512, 512)
        E, R, K = (8, 64, 128)
        SCALE = 64.0 / 64.0
        MULTIPLIER = 1.0
        base = jnp.einsum('bsi,oi->bso', x, W_org)
        q = jnp.einsum('bi,ki->bk', x.mean(axis=1), Wq)
        scores = jnp.einsum('bk,ek->be', q, lora_keys) / math.sqrt(K)
        coeffs = jax.nn.softmax(scores, axis=-1)
        h = jnp.einsum('bsi,eir->bser', x, lora_down)
        delta = jnp.einsum('be,bser,ero->bso', coeffs, h, lora_up)
        return base + delta * (SCALE * MULTIPLIER)
    x = L0_attn_hidden_states
    x = _layernorm(x + _L0_attn_ref(x, L0_attn_wq, L0_attn_bq, L0_attn_wk, L0_attn_bk, L0_attn_wv, L0_attn_bv, L0_attn_wl, L0_attn_bl), axis=-1)
    x = _layernorm(x + _L0_ffn_ref(x, L0_ffn_W_org, L0_ffn_lora_down, L0_ffn_lora_up, L0_ffn_lora_keys, L0_ffn_Wq), axis=-1)
    return x

_drawn_inputs = setup_inputs


def setup_inputs(seed=0):
    import zlib

    import numpy as np

    out = dict(_drawn_inputs(seed))
    spreads = {}
    factors = {'L0_attn_wq': 3.133,
     'L0_attn_bq': 8.0,
     'L0_attn_wk': 2.825,
     'L0_attn_bk': 8.0,
     'L0_attn_bv': 8.0,
     'L0_ffn_lora_keys': 8.0,
     'L0_ffn_Wq': 8.0}
    for name, (base, spread) in spreads.items():
        noise = np.random.default_rng([zlib.crc32(name.encode()), seed]).standard_normal(out[name].shape)
        drawn = base * np.exp(spread * noise) if base else spread * noise
        out[name] = jnp.asarray(drawn.astype(out[name].dtype))
    for name, factor in factors.items():
        out[name] = (out[name] * factor).astype(out[name].dtype)
    return out
```

```python
from contextlib import ExitStack

import concourse.bass as bass
from concourse import mybir

ALU = mybir.AluOpType
ACT = mybir.ActivationFunctionType
F32 = mybir.dt.float32
AX_X = mybir.AxisListType.X

P = 128
Q = 32
NQ = P // Q
LN_EPS = 1e-5


def wait_if_any(engine, semaphore, value):
    if not isinstance(value, int) or value > 0:
        engine.wait_ge(semaphore, value)


def at(b, per_batch, k):
    return b * per_batch + k


def seq_postln_kernel(nc, x, wq, bq, wk, bk, wv, bv, w_org, lora_down, lora_up, lora_keys, w_gate, out):
    B, S, D = x.shape
    E, _, R = lora_down.shape
    KD = lora_keys.shape[1]
    C = D // P
    U = S // P
    H = Q
    HD = D // H
    DA = HD + 1
    J = Q
    G = J // NQ
    HALF = G // 2
    M = E * R // P
    EPC = P // R
    assert D == 512 and H * HD == D and U == 2 and KD == P and E * R == D and EPC == 2
    SCORE_SCALE = float(HD) ** -0.5
    GATE_SCALE = 1.0 / (S * float(KD) ** 0.5)

    ctx = ExitStack()
    with ctx:
        def sb(name, shape):
            return ctx.enter_context(nc.sbuf_tensor(name, shape, F32))

        def psum(name, shape):
            return ctx.enter_context(nc.psum_tensor(name, shape, F32))

        def sem(name):
            return ctx.enter_context(nc.semaphore(name))

        ident = sb("ident", [P, P])
        minus_half = sb("minus_half", [P, U])
        eps = sb("eps", [P, U])
        w_T = sb("w_T", [P, 4, C, D])
        down = sb("down", [P, C, E * R])
        up = sb("up", [P, M, D])
        bias = sb("bias", [P, 3, D])
        keys = sb("keys", [E, KD])
        keys_T = sb("keys_T", [KD, E])
        gate_raw = sb("gate_raw", [KD, D])
        gate = sb("gate", [P, C, E])

        x_in = sb("x_in", [P, U, D])
        x_res = sb("x_res", [P, U, D])
        x_T = sb("x_T", [P, C, S])
        x_Tv = sb("x_Tv", [P, U, C, P])
        qk_tok = sb("qk_tok", [P, 2, U, H, Q])
        v_tok = sb("v_tok", [P, U, D])
        q_T = sb("q_T", [P, U, J, H])
        k_T = sb("k_T", [P, U, J, H])
        v_T = sb("v_T", [P, U, HD, J])
        k_diag = sb("k_diag", [P, NQ, U, J, H])
        v_diag = sb("v_diag", [P, U, NQ, DA, J])
        probs = sb("probs", [P, U, J, H])
        probs_T = sb("probs_T", [P, U, J, H])
        row_max = sb("row_max", [P, U, J])
        ctx_tok = sb("ctx_tok", [P, U, DA, H])
        inv_sum = sb("inv_sum", [P, U, H])
        pre1 = sb("pre1", [P, U, D])
        x1 = sb("x1", [P, U, D])
        x1_T = sb("x1_T", [P, C, S])
        x1_sum = sb("x1_sum", [P, C])
        h_T = sb("h_T", [P, M, S])
        pre2 = sb("pre2", [P, U, D])
        y = sb("y", [P, U, D])
        gmax = sb("gmax", [P, 1])
        gbias = sb("gbias", [P, 1])
        gexp = sb("gexp", [P, E])
        gsum = sb("gsum", [P, 1])
        ginv = sb("ginv", [P, 1])
        coef = sb("coef", [P, M])
        stats = sb("stats", [P, 2, U, 6])
        moments = sb("moments", [P, 2, U, 2])
        var_eps = sb("var_eps", [P, 2, U])
        rstd = sb("rstd", [P, 2, U])
        w_raw = k_diag[:].rearrange("p r u j h -> p (r u j h)").rearrange("p (w c i) -> p w c i", w=4, c=C)

        ps_lin = psum("ps_lin", [P, 2, D])
        ps_att = psum("ps_att", [P, U, 2, 512])
        ps_turn = psum("ps_turn", [P, 2, 512])

        x_loaded = sem("x_loaded")
        w_loaded = [sem(f"w_loaded{n}") for n in range(4)]
        bias_loaded = sem("bias_loaded")
        gate_loaded = sem("gate_loaded")
        lora_loaded = sem("lora_loaded")
        consts_zero = sem("consts_zero")
        ident_ready = sem("ident_ready")
        pads_ready = sem("pads_ready")
        diag_zero = sem("diag_zero")
        diag_ready = sem("diag_ready")
        ones_placed = sem("ones_placed")
        w_turned = sem("w_turned")
        w_kept_act = sem("w_kept_act")
        w_kept_dve = sem("w_kept_dve")
        gate_made = sem("gate_made")
        gate_kept = sem("gate_kept")
        xT_made = sem("xT_made")
        xT_kept = sem("xT_kept")
        xTv_kept = sem("xTv_kept")
        x_res_kept = sem("x_res_kept")
        proj_made = sem("proj_made")
        proj_kept = sem("proj_kept")
        biased = sem("biased")
        qk_turned = sem("qk_turned")
        v_turned = sem("v_turned")
        k_placed = sem("k_placed")
        v_placed = sem("v_placed")
        scores_made = sem("scores_made")
        max_made = sem("max_made")
        shifted = sem("shifted")
        exp_made = sem("exp_made")
        probs_turned = sem("probs_turned")
        ctx_made = sem("ctx_made")
        ctx_turned = sem("ctx_turned")
        inv_made = sem("inv_made")
        attn_made = sem("attn_made")
        pre1_made = sem("pre1_made")
        x1_made = sem("x1_made")
        x1T_made = sem("x1T_made")
        x1T_kept = sem("x1T_kept")
        gscore_made = sem("gscore_made")
        gmax_made = sem("gmax_made")
        gbias_made = sem("gbias_made")
        gexp_made = sem("gexp_made")
        ginv_made = sem("ginv_made")
        coef_made = sem("coef_made")
        h_made = sem("h_made")
        h_kept = sem("h_kept")
        out_made = sem("out_made")
        pre2_made = sem("pre2_made")
        y_made = sem("y_made")
        y_stored = sem("y_stored")
        y_free = sem("y_free")
        moments_made = [sem(f"moments_made{n}") for n in (1, 2)]
        eps_added = [sem(f"eps_added{n}") for n in (1, 2)]
        rstd_made = [sem(f"rstd_made{n}") for n in (1, 2)]

        block = ctx.enter_context(nc.Block())

        @block.sync
        def _(sp):
            def place_k(scores_read, both_turned):
                wait_if_any(sp, scores_made, scores_read)
                sp.wait_ge(qk_turned, both_turned)
                for r in range(NQ):
                    sp.dma_start(k_diag[Q * r:Q * r + HD, r, :, :, :],
                                 k_T[Q * r:Q * r + HD, :, :, :]).then_inc(k_placed, 16)

            def place_v(context_read, both_turned):
                sp.wait_ge(v_turned, both_turned)
                wait_if_any(sp, ctx_made, context_read)
                for c in range(NQ):
                    sp.dma_start(v_diag[Q * c:Q * c + Q, :, c, 0:HD, :],
                                 v_T[Q * c:Q * c + Q, :, :, :]).then_inc(v_placed, 16)

            for n, w in enumerate((wq, wk, wv, w_org)):
                sp.dma_start(w_raw[:, n], w.rearrange("(c p) i -> p c i", p=P)).then_inc(w_loaded[n], 16)
            sp.dma_start(up[:], lora_up.rearrange("e r o -> (e r) o").rearrange("(m p) o -> p m o", p=P))\
                .then_inc(lora_loaded, 16)
            for c in range(C):
                sp.dma_start(down[:, c, :].rearrange("p (e r) -> p e r", e=E),
                             lora_down[:, c * P:(c + 1) * P, :].rearrange("e p r -> p e r")).then_inc(lora_loaded, 16)
            sp.wait_ge(diag_ready, 1)
            place_k(0, 2 * U)
            place_v(0, U)
            with sp.Fori(1, B) as b:
                place_k(at(b, U, 0), at(b, 2 * U, 2 * U))
                place_v(at(b, U, 0), at(b, U, U))

        @block.gpsimd
        def _(pool):
            def add_bias(b, n, target, shape):
                pool.wait_ge(proj_kept, at(b, 3 * U, n + 1))
                nc.gpsimd.tensor_tensor(target, target, shape, ALU.add).then_inc(biased, 1)

            def add_biases(b):
                for u in range(U):
                    for w in range(2):
                        add_bias(b, 2 * u + w, qk_tok[:, w, u, :, 0:HD],
                                 bias[:, w, :].rearrange("p (h d) -> p h d", h=H))
                for u in range(U):
                    add_bias(b, 2 * U + u, v_tok[:, u, :], bias[:, 2, :])

            def load_x(b):
                pool.wait_ge(xT_made, at(b, U, 0))
                pool.wait_ge(x_res_kept, b)
                pool.dma_start(x_in[:], x[b].rearrange("(u p) i -> p u i", p=P)).then_inc(x_loaded, 16)

            def store_y(b):
                pool.wait_ge(y_made, at(b, U, U))
                pool.dma_start(out[b].rearrange("(u p) o -> p u o", p=P), y[:]).then_inc(y_stored, 16)
                pool.wait_ge(y_stored, at(b, 16, 16))
                pool.sem_inc(y_free, 1)

            def inverse_deviation(b, n):
                pool.wait_ge(moments_made[n], at(b, U, U))
                nc.gpsimd.tensor_tensor(var_eps[:, n, :], moments[:, n, :, 1], eps[:], ALU.add)\
                    .then_inc(eps_added[n], 1)
                pool.wait_ge(eps_added[n], b + 1)
                nc.gpsimd.tensor_tensor(rstd[:, n, :], var_eps[:, n, :], minus_half[:], ALU.pow)\
                    .then_inc(rstd_made[n], 1)

            pool.sem_inc(y_free, 1)
            pool.dma_start(x_in[:], x[0].rearrange("(u p) i -> p u i", p=P)).then_inc(x_loaded, 16)
            nc.gpsimd.memset(ident[:], 0.0).then_inc(consts_zero, 1)
            nc.gpsimd.memset(minus_half[:], -0.5).then_inc(consts_zero, 1)
            nc.gpsimd.memset(eps[:], LN_EPS).then_inc(consts_zero, 1)
            pool.wait_ge(consts_zero, 3)
            nc.gpsimd.affine_select(out=ident[:], in_=ident[:], compare_op=ALU.not_equal, fill=1.0, base=0,
                                    pattern=[[-1, P]], channel_multiplier=1).then_inc(ident_ready, 1)
            nc.gpsimd.memset(qk_tok[:], 0.0).then_inc(pads_ready, 1)
            nc.gpsimd.memset(v_diag[:], 0.0).then_inc(diag_zero, 1)
            pool.wait_ge(bias_loaded, 3 * 16)
            add_biases(0)
            pool.wait_ge(w_turned, 4 * C)
            nc.gpsimd.memset(k_diag[:], 0.0).then_inc(diag_ready, 1)
            load_x(1)
            with pool.Fori(1, B - 1) as b:
                inverse_deviation(b - 1, 0)
                add_biases(b)
                load_x(b + 1)
                inverse_deviation(b - 1, 1)
                store_y(b - 1)
            inverse_deviation(B - 2, 0)
            add_biases(B - 1)
            inverse_deviation(B - 2, 1)
            store_y(B - 2)
            inverse_deviation(B - 1, 0)
            inverse_deviation(B - 1, 1)
            store_y(B - 1)

        @block.scalar
        def _(act):
            def keep_weight(n):
                act.wait_ge(w_turned, n + 1)
                nc.scalar.copy(w_T[:, n // C, n % C, :], ps_att[:, n % 4 // 2, n % 2, :]).then_inc(w_kept_act, 1)

            def keep_x_T(b):
                for u in range(U):
                    act.wait_ge(xT_made, at(b, U, u + 1))
                    nc.scalar.copy(x_T[:, :, u * P:(u + 1) * P],
                                   ps_turn[:, u, :].rearrange("p (c t) -> p c t", c=C)).then_inc(xT_kept, 1)
                for u in range(U):
                    nc.scalar.copy(x_Tv[:, u].rearrange("p c (k m) -> p c k m", k=NQ),
                                   ps_turn[:, u, :].rearrange("p (c m k) -> p c k m", c=C, k=NQ))\
                        .then_inc(xTv_kept, 1)

            def keep_residual(b):
                wait_if_any(act, pre1_made, b)
                act.wait_ge(x_loaded, at(b, 16, 16))
                nc.scalar.copy(x_res[:], x_in[:]).then_inc(x_res_kept, 1)

            def keep_projection(b, n, target, view):
                act.wait_ge(proj_made, at(b, 3 * U, n + 1))
                nc.scalar.copy(target, view).then_inc(proj_kept, 1)

            def keep_qk(b):
                wait_if_any(act, qk_turned, at(b, 2 * U, 0))
                for u in range(U):
                    for w in range(2):
                        keep_projection(b, 2 * u + w, qk_tok[:, w, u, :, 0:HD],
                                        ps_lin[:, w, :].rearrange("p (h d) -> p h d", h=H))

            def keep_v(b):
                wait_if_any(act, v_turned, at(b, U, 0))
                for u in range(U):
                    keep_projection(b, 2 * U + u, v_tok[:, u, :], ps_lin[:, u, :])

            def keep_x1_T(b):
                for c in range(C):
                    act.wait_ge(x1T_made, at(b, 2, c // 2 + 1))
                    nc.scalar.activation(x1_T[:, c, :], ps_turn[:, c // 2, c % 2 * S:(c % 2 + 1) * S], ACT.Copy,
                                         accum_out=x1_sum[:, c:c + 1]).then_inc(x1T_kept, 1)

            def gate_exp(b):
                act.wait_ge(gbias_made, b + 1)
                nc.scalar.activation(gexp[:], ps_lin[:, 1, 0:E], ACT.Exp, bias=gbias[:], scale=GATE_SCALE,
                                     accum_out=gsum[:]).then_inc(gexp_made, 1)

            def exps(b):
                for u in range(U):
                    act.wait_ge(shifted, at(b, U, u + 1))
                    nc.scalar.activation(probs[:, u], probs[:, u], ACT.Exp, scale=SCORE_SCALE).then_inc(exp_made, 1)

            def keep_h(b):
                act.wait_ge(out_made, at(b, U, U))
                act.wait_ge(coef_made, at(b, EPC, EPC))
                for m in range(M):
                    act.wait_ge(h_made, at(b, M // 2, m // 2 + 1))
                    nc.scalar.mul(h_T[:, m, :], ps_turn[:, m // 2, m % 2 * S:(m % 2 + 1) * S],
                                  coef[:, m:m + 1]).then_inc(h_kept, 1)

            act.sem_inc(h_kept, M)
            for n, v in enumerate((bq, bk, bv)):
                act.dma_start(bias[:, n, :], v.partition_broadcast(P)).then_inc(bias_loaded, 16)
            act.dma_start(keys[:], lora_keys).then_inc(gate_loaded, 16)
            act.dma_start(gate_raw[:], w_gate).then_inc(gate_loaded, 16)
            keep_x_T(0)
            keep_residual(0)
            for n in range(0, 2 * C, 2):
                keep_weight(n)
            act.wait_ge(pads_ready, 1)
            keep_qk(0)
            for n in range(2 * C, 3 * C):
                keep_weight(n)
            keep_v(0)
            for n in range(3 * C, 4 * C):
                keep_weight(n)
            exps(0)
            with act.Fori(1, B) as b:
                keep_x_T(b)
                keep_qk(b)
                keep_residual(b)
                keep_x1_T(b - 1)
                keep_v(b)
                gate_exp(b - 1)
                exps(b)
                keep_h(b - 1)
            keep_x1_T(B - 1)
            gate_exp(B - 1)
            keep_h(B - 1)

        @block.vector
        def _(dve):
            def keep_weight(n):
                dve.wait_ge(w_turned, n + 1)
                nc.vector.tensor_copy(w_T[:, n // C, n % C, :], ps_att[:, n % 4 // 2, n % 2, :])\
                    .then_inc(w_kept_dve, 1)

            def turn_qk(b, first):
                if not first:
                    dve.wait_ge(scores_made, at(b, U, 0))
                    dve.wait_ge(k_placed, at(b, NQ * 16, 0))
                for u in range(U):
                    for w, turned in enumerate((q_T, k_T)):
                        dve.wait_ge(biased, at(b, 3 * U, 2 * u + w + 1))
                        nc.vector.transpose(turned[:, u].rearrange("p j h -> p h j"), qk_tok[:, w, u])\
                            .then_inc(qk_turned, 1)

            def turn_v(b, first):
                if not first:
                    dve.wait_ge(v_placed, at(b, NQ * 16, 0))
                for u in range(U):
                    dve.wait_ge(biased, at(b, 3 * U, 2 * U + u + 1))
                    nc.vector.transpose(v_T[:, u], v_tok[:, u, :].rearrange("p (t d) -> p d t", d=HD))\
                        .then_inc(v_turned, 1)

            def shift_scores(b):
                for u in range(U):
                    scores = ps_att[:, u].rearrange("p a (m t) -> p (a m) t", t=H)
                    dve.wait_ge(scores_made, at(b, U, u + 1))
                    nc.vector.reduce_max(row_max[:, u, :], scores, AX_X).then_inc(max_made, 1)
                    dve.wait_ge(max_made, at(b, U, u + 1))
                    nc.vector.tensor_tensor(probs[:, u], scores, row_max[:, u, :].unsqueeze(2).to_broadcast([P, J, H]),
                                            ALU.subtract).then_inc(shifted, 1)

            def turn_probs(b):
                for u in range(U):
                    dve.wait_ge(exp_made, at(b, U, u + 1))
                    nc.vector.transpose(probs_T[:, u], probs[:, u]).then_inc(probs_turned, 1)

            def moments_of(b, n, source, made, count):
                dve.wait_ge(made, b + count)
                for u in range(U):
                    nc.vector.bn_stats(stats[:, n, u, :], source[:, u, :])
                dve.drain()
                for u in range(U):
                    nc.vector.bn_aggr(moments[:, n, u, :], stats[:, n, u, :]).then_inc(moments_made[n], 1)

            def normalise(b, n, target, source, made):
                dve.wait_ge(moments_made[n], at(b, U, U))
                dve.wait_ge(rstd_made[n], b + 1)
                for u in range(U):
                    nc.vector.tensor_scalar(target[:, u, :], source[:, u, :], moments[:, n, u, 0:1],
                                            rstd[:, n, u:u + 1], ALU.subtract, ALU.mult).then_inc(made, 1)

            def first_layernorm(b):
                for u in range(U):
                    dve.wait_ge(ctx_made, at(b, U, u + 1))
                    source = ps_att[:, u, :, 0:HALF * NQ * DA].rearrange("p a (j d) -> p d a j", d=DA)
                    nc.vector.transpose(ctx_tok[:, u], source).then_inc(ctx_turned, 1)
                dve.wait_ge(ctx_turned, at(b, U, U))
                nc.vector.reciprocal(inv_sum[:], ctx_tok[:, :, HD, :]).then_inc(inv_made, 1)
                dve.wait_ge(inv_made, b + 1)
                nc.vector.tensor_tensor(pre1[:].rearrange("p u (h d) -> p u h d", h=H),
                                        ctx_tok[:, :, 0:HD, :].rearrange("p u d h -> p u h d"),
                                        inv_sum[:].unsqueeze(3).to_broadcast([P, U, H, HD]),
                                        ALU.mult).then_inc(attn_made, 1)
                dve.wait_ge(attn_made, b + 1)
                dve.wait_ge(x_res_kept, b + 1)
                nc.vector.tensor_tensor(pre1[:], pre1[:], x_res[:], ALU.add).then_inc(pre1_made, 1)
                moments_of(b, 0, pre1, pre1_made, 1)
                normalise(b, 0, x1, pre1, x1_made)

            def gate_shift(b):
                dve.wait_ge(gscore_made, b + 1)
                nc.vector.reduce_max(gmax[:], ps_lin[:, 1, 0:E], AX_X).then_inc(gmax_made, 1)
                dve.wait_ge(gmax_made, b + 1)
                nc.vector.tensor_scalar(gbias[:], gmax[:], -GATE_SCALE, None, ALU.mult).then_inc(gbias_made, 1)

            def gate_coefficients(b):
                dve.wait_ge(gexp_made, b + 1)
                nc.vector.reciprocal(ginv[:], gsum[:]).then_inc(ginv_made, 1)
                dve.wait_ge(ginv_made, b + 1)
                dve.wait_ge(h_kept, at(b, M, M))
                for e in range(EPC):
                    rows = slice(R * e, R * (e + 1))
                    nc.vector.tensor_scalar(coef[rows, :], gexp[rows, e:E:EPC], ginv[rows, :], None, ALU.mult)\
                        .then_inc(coef_made, 1)

            def second_layernorm(b):
                for u in range(U):
                    dve.wait_ge(out_made, at(b, U, U + u + 1))
                    ins = nc.vector.tensor_tensor(pre2[:, u, :], ps_lin[:, u, :], x1[:, u, :], ALU.add)
                ins.then_inc(pre2_made, 1)
                moments_of(b, 1, pre2, pre2_made, 2)
                dve.wait_ge(y_free, b + 1)
                normalise(b, 1, y, pre2, y_made)

            dve.sem_inc(pre2_made, 1)
            dve.wait_ge(diag_zero, 1)
            for c in range(NQ):
                nc.vector.memset(v_diag[Q * c:Q * c + Q, :, c, HD, :], 1.0).then_inc(ones_placed, 1)
            for n in range(1, 2 * C, 2):
                keep_weight(n)
            turn_qk(0, True)
            turn_v(0, True)
            dve.wait_ge(gate_made, 1)
            nc.vector.tensor_copy(keys_T[:], ps_turn[:, 0, 0:E]).then_inc(gate_kept, 1)
            dve.wait_ge(gate_made, 2)
            nc.vector.tensor_copy(gate[:], ps_turn[:, 1, 0:C * E].rearrange("p (c e) -> p c e", c=C))\
                .then_inc(gate_kept, 1)
            shift_scores(0)
            turn_probs(0)
            with dve.Fori(1, B) as b:
                first_layernorm(b - 1)
                turn_qk(b, False)
                turn_v(b, False)
                gate_shift(b - 1)
                shift_scores(b)
                gate_coefficients(b - 1)
                turn_probs(b)
                second_layernorm(b - 1)
            first_layernorm(B - 1)
            gate_shift(B - 1)
            gate_coefficients(B - 1)
            second_layernorm(B - 1)

        @block.tensor
        def _(pe):
            def turn_weight(w):
                pe.wait_ge(w_loaded[w], 16)
                for c in range(C):
                    n = w * C + c
                    if n >= 4:
                        if n - 4 >= 2 * C:
                            pe.wait_ge(w_kept_act, C + n - 4 - 2 * C + 1)
                        elif n % 2:
                            pe.wait_ge(w_kept_dve, (n - 4) // 2 + 1)
                        else:
                            pe.wait_ge(w_kept_act, (n - 4) // 2 + 1)
                    bank = ps_att[:, n % 4 // 2, n % 2, :]
                    for o in range(C):
                        ins = nc.tensor.transpose(bank[:, o * P:(o + 1) * P], w_raw[:, w, o, c * P:(c + 1) * P],
                                                  ident[:])
                    ins.then_inc(w_turned, 1)

            def turn_x(b):
                pe.wait_ge(x_loaded, at(b, 16, 16))
                for u in range(U):
                    for c in range(C):
                        ins = nc.tensor.transpose(ps_turn[:, u, c * P:(c + 1) * P], x_in[:, u, c * P:(c + 1) * P],
                                                  ident[:])
                    ins.then_inc(xT_made, 1)

            def project_qk(b, tiles, first=False):
                for u in tiles:
                    pe.wait_ge(xT_kept, at(b, U, u + 1))
                    for w in range(2):
                        if u == 0 and not first:
                            pe.wait_ge(pre2_made, b)
                        if u > 0:
                            pe.wait_ge(proj_kept, at(b, 3 * U, 2 * u + w - 1))
                        for c in range(C):
                            ins = nc.tensor.matmul(ps_lin[:, w, :], x_T[:, c, u * P:(u + 1) * P], w_T[:, w, c, :],
                                                   start=(c == 0), stop=(c == C - 1))
                        ins.then_inc(proj_made, 1)

            def project_v(b):
                for u in range(U):
                    pe.wait_ge(xTv_kept, at(b, U, u + 1))
                    pe.wait_ge(proj_kept, at(b, 3 * U, 2 * U + u - 1))
                    for c in range(C):
                        ins = nc.tensor.matmul(ps_lin[:, u, :], x_Tv[:, u, c, :], w_T[:, 2, c, :],
                                               start=(c == 0), stop=(c == C - 1))
                    ins.then_inc(proj_made, 1)

            def scores(b, first):
                pe.wait_ge(k_placed, at(b, NQ * 16, NQ * 16))
                for u in range(U):
                    if not first:
                        pe.wait_ge(ctx_turned, at(b - 1, U, u + 1))
                    for g in range(G):
                        for c in range(NQ):
                            j = NQ * g + c
                            cols = slice(g % HALF * P, (g % HALF + 1) * P)
                            ins = nc.tensor.matmul(ps_att[Q * c:Q * c + Q, u, g // HALF, cols]
                                                   .rearrange("h (r t) -> h r t", r=NQ),
                                                   q_T[:, u, j, :], k_diag[:, :, u, j, :], start=True, stop=True)
                    ins.then_inc(scores_made, 1)

            def context(b):
                pe.wait_ge(v_placed, at(b, NQ * 16, NQ * 16))
                for u in range(U):
                    pe.wait_ge(probs_turned, at(b, U, u + 1))
                    for g in range(G):
                        for r in range(NQ):
                            cols = slice(g % HALF * NQ * DA, (g % HALF + 1) * NQ * DA)
                            ins = nc.tensor.matmul(ps_att[Q * r:Q * r + Q, u, g // HALF, cols]
                                                   .rearrange("h (c d) -> h c d", c=NQ),
                                                   probs_T[:, u, NQ * g + r, :], v_diag[:, u, :, :, G * r + g],
                                                   start=True, stop=True)
                    ins.then_inc(ctx_made, 1)

            def turn_x1(b, x_kept):
                pe.wait_ge(xTv_kept, x_kept)
                pe.wait_ge(x1_made, at(b, U, U))
                for c in range(C):
                    for u in range(U):
                        at_ = c % 2 * S + u * P
                        ins = nc.tensor.transpose(ps_turn[:, c // 2, at_:at_ + P], x1[:, u, c * P:(c + 1) * P],
                                                  ident[:])
                    if c % 2:
                        ins.then_inc(x1T_made, 1)

            def gate_scores(b, projected):
                pe.wait_ge(proj_kept, projected)
                pe.wait_ge(x1T_kept, at(b, C, C))
                for r in range(NQ):
                    for c in range(C):
                        ins = nc.tensor.matmul(ps_lin[Q * r:Q * r + Q, 1, 0:E], x1_sum[:, c:c + 1].to_broadcast([P, Q]),
                                               gate[:, c, :], start=(c == 0), stop=(c == C - 1))
                ins.then_inc(gscore_made, 1)

            def feed_forward(b):
                for m in range(M):
                    for c in range(C):
                        ins = nc.tensor.matmul(ps_turn[:, m // 2, m % 2 * S:(m % 2 + 1) * S],
                                               down[:, c, m * P:(m + 1) * P], x1_T[:, c, :],
                                               start=(c == 0), stop=(c == C - 1))
                    if m % 2:
                        ins.then_inc(h_made, 1)
                pe.wait_ge(gexp_made, b + 1)
                for u in range(U):
                    for c in range(C):
                        nc.tensor.matmul(ps_lin[:, u, :], x1_T[:, c, u * P:(u + 1) * P], w_T[:, 3, c, :],
                                         start=(c == 0), stop=False)
                    for m in range(M):
                        if u == 0:
                            pe.wait_ge(h_kept, at(b, M, M + m + 1))
                        ins = nc.tensor.matmul(ps_lin[:, u, :], h_T[:, m, u * P:(u + 1) * P], up[:, m, :],
                                               start=False, stop=(m == M - 1))
                    ins.then_inc(out_made, 1)

            pe.sem_inc(out_made, U)
            pe.wait_ge(ident_ready, 1)
            turn_x(0)
            turn_weight(0)
            turn_weight(1)
            pe.wait_ge(w_kept_act, C)
            pe.wait_ge(w_kept_dve, C)
            project_qk(0, range(U), first=True)
            turn_weight(2)
            pe.wait_ge(w_kept_act, 2 * C)
            project_v(0)
            turn_weight(3)
            pe.wait_ge(gate_loaded, 2 * 16)
            nc.tensor.transpose(ps_turn[:, 0, 0:E], keys[:], ident[0:E, 0:E]).then_inc(gate_made, 1)
            pe.wait_ge(gate_kept, 1)
            for c in range(C):
                ins = nc.tensor.matmul(ps_turn[:, 1, c * E:(c + 1) * E], gate_raw[:, c * P:(c + 1) * P], keys_T[:],
                                       start=True, stop=True)
            ins.then_inc(gate_made, 1)
            pe.wait_ge(w_kept_act, 3 * C)
            scores(0, True)
            pe.wait_ge(gate_kept, 2)
            pe.wait_ge(lora_loaded, (1 + C) * 16)
            pe.wait_ge(ones_placed, NQ)
            with pe.Fori(1, B) as b:
                pe.wait_ge(h_kept, at(b, M, 0))
                turn_x(b)
                project_qk(b, [0])
                context(b - 1)
                project_qk(b, [1])
                turn_x1(b - 1, at(b, U, U))
                project_v(b)
                gate_scores(b - 1, at(b, 3 * U, 3 * U))
                scores(b, False)
                feed_forward(b - 1)
            context(B - 1)
            turn_x1(B - 1, at(B - 1, U, U))
            gate_scores(B - 1, at(B - 1, 3 * U, 3 * U))
            feed_forward(B - 1)


_INS = ['L0_attn_hidden_states', 'L0_attn_wq', 'L0_attn_bq', 'L0_attn_wk', 'L0_attn_bk', 'L0_attn_wv', 'L0_attn_bv',
        'L0_ffn_W_org', 'L0_ffn_lora_down', 'L0_ffn_lora_up', 'L0_ffn_lora_keys', 'L0_ffn_Wq']


def kernel(**inputs):
    import numpy as _np
    import concourse.bacc as _bacc
    from concourse import mybir as _mybir
    from concourse.bass_utils import run_bass_kernel_spmd as _run

    nc = _bacc.Bacc("TRN2", target_bir_lowering=False, num_devices=1)
    arrays, args = {}, []
    for name in _INS:
        a = _np.ascontiguousarray(inputs[name])
        arrays[f"in_{name}_dram"] = a
        args.append(nc.dram_tensor(f"in_{name}_dram", a.shape, _mybir.dt.from_np(a.dtype), kind="ExternalInput").ap())
    shape = inputs['L0_attn_hidden_states'].shape
    args.append(nc.dram_tensor("out_0_dram", shape, _mybir.dt.float32, kind="ExternalOutput").ap())
    seq_postln_kernel(nc, *args)
    r = _run(nc, [arrays], core_ids=[0])
    return r.results[0]["out_0_dram"]
```

```python
from contextlib import ExitStack

import concourse.bass as bass
from concourse import mybir

ALU = mybir.AluOpType
ACT = mybir.ActivationFunctionType
F32 = mybir.dt.float32
F32R = mybir.dt.float32r
AX_X = mybir.AxisListType.X

P = 128
Q = 32
NQ = P // Q
LN_EPS = 1e-5


def wait_if_any(engine, semaphore, value):
    if not isinstance(value, int) or value > 0:
        engine.wait_ge(semaphore, value)


def at(b, per_batch, k):
    return b * per_batch + k


def seq_postln_kernel(nc, x, wq, bq, wk, bk, wv, bv, w_org, lora_down, lora_up, lora_keys, w_gate, out):
    B, S, D = x.shape
    E, _, R = lora_down.shape
    KD = lora_keys.shape[1]
    C = D // P
    U = S // P
    H = Q
    HD = D // H
    DA = HD + 1
    J = Q
    G = J // NQ
    HALF = G // 2
    M = E * R // P
    EPC = P // R
    assert D == 512 and H * HD == D and U == 2 and KD == P and E * R == D and EPC == 2
    SCORE_SCALE = float(HD) ** -0.5
    GATE_SCALE = 1.0 / (S * float(KD) ** 0.5)

    ctx = ExitStack()
    with ctx:
        def sb(name, shape, dtype=F32):
            return ctx.enter_context(nc.sbuf_tensor(name, shape, dtype))

        def flat(tensor):
            names = "abcd"[:len(tensor.shape) - 1]
            return tensor[:].rearrange(f"p {' '.join(names)} -> p ({' '.join(names)})")

        def psum(name, shape):
            return ctx.enter_context(nc.psum_tensor(name, shape, F32))

        def sem(name):
            return ctx.enter_context(nc.semaphore(name))

        ident = sb("ident", [P, P])
        minus_half = sb("minus_half", [P, 1])
        eps = sb("eps", [P, 1])
        w_hi = sb("w_hi", [P, 4, C, D], F32R)
        w_lo = sb("w_lo", [P, 4, C, D], F32R)
        down_hi = sb("down_hi", [P, C, E * R], F32R)
        down_lo = sb("down_lo", [P, C, E * R], F32R)
        up_hi = sb("up_hi", [P, M, D], F32R)
        up_lo = sb("up_lo", [P, M, D], F32R)
        bias = sb("bias", [P, 3, D])
        keys = sb("keys", [E, KD])
        keys_T = sb("keys_T", [KD, E])
        gate_raw = sb("gate_raw", [KD, D])
        gate = sb("gate", [P, C, E])

        x_in = sb("x_in", [P, U, D])
        feat_hi = sb("feat_hi", [P, C, S], F32R)
        feat_lo = sb("feat_lo", [P, C, S], F32R)
        aux_hi = sb("aux_hi", [P, C * S], F32R)
        aux_lo = sb("aux_lo", [P, C * S], F32R)
        xv_hi, xv_lo = (t[:].rearrange("p (u c t) -> p u c t", u=U, c=C) for t in (aux_hi, aux_lo))
        h_hi, h_lo = (t[:].rearrange("p (m t) -> p m t", m=M) for t in (aux_hi, aux_lo))
        qk_tok = sb("qk_tok", [P, 2, U, D + Q - HD])
        q_T = sb("q_T", [P, U, J, H])
        k_T = sb("k_T", [P, U, J, H])
        v_T = sb("v_T", [P, U, HD, J])
        k_diag = sb("k_diag", [P, NQ, J, H])
        v_diag = sb("v_diag", [P, NQ, DA, J])
        probs = sb("probs", [P, U, J, H])
        probs_T = sb("probs_T", [P, U, J, H])
        row_max = sb("row_max", [P, U, J])
        ctx_tok = [probs_T[:, u].rearrange("p j h -> p (j h)")[:, 0:DA * H].rearrange("p (d h) -> p d h", h=H)
                   for u in range(U)]
        inv_sum = sb("inv_sum", [P, U, H])
        resid = sb("resid", [P, 2, U, D])
        pre1, x1 = resid[:, 0], resid[:, 1]
        tok = sb("tok", [P, U, D])
        v_tok, pre2, y = tok, tok, tok
        x1_sum = sb("x1_sum", [P, C])
        gmax = sb("gmax", [P, 1])
        gbias = sb("gbias", [P, 1])
        gexp = sb("gexp", [P, E])
        gsum = sb("gsum", [P, 1])
        ginv = sb("ginv", [P, 1])
        coef = sb("coef", [P, M])
        stats = sb("stats", [P, 2, U, 6])
        moments = sb("moments", [P, 2, U, 2])
        var_eps = sb("var_eps", [P, 2, U])
        rstd = sb("rstd", [P, 2, U])
        w_raw = [flat(k_diag)[:, 0:C * D], flat(k_diag)[:, C * D:2 * C * D], flat(v_diag)[:, 0:C * D], flat(probs_T)]
        w_raw = [t.rearrange("p (c i) -> p c i", c=C) for t in w_raw]
        down_raw = flat(probs).rearrange("p (c i) -> p c i", c=C)
        up_raw, MU = x1, M // 2

        ps_lin = psum("ps_lin", [P, 2, D])
        ps_att = psum("ps_att", [P, U, 2, 512])
        ps_turn = psum("ps_turn", [P, 2, 512])

        WEIGHT_BANKS = (4, 4, 4, 2)

        def weight_bank(n):
            k = n % 4 if n < 3 * C else 2 + n % 2
            return ps_att[:, k // 2, k % 2, :]

        def sems(names):
            return [sem(name) for name in names.split()]

        x_loaded, bias_loaded, gate_loaded, down_loaded, up_loaded = sems(
            "x_loaded bias_loaded gate_loaded down_loaded up_loaded")
        wq_loaded = [sem(f"wq_loaded{c}") for c in range(C)]
        w_loaded = [None] + [sem(f"w_loaded{n}") for n in range(1, 4)]
        consts_set, ident_ready, pads_ready, k_diag_zero, v_diag_zero, ones_placed = sems(
            "consts_set ident_ready pads_ready k_diag_zero v_diag_zero ones_placed")
        w_turned, w_hi_made, w_lo_made = sems("w_turned w_hi_made w_lo_made")
        down_hi_made, down_lo_made, up_hi_made, up_lo_made = sems("down_hi_made down_lo_made up_hi_made up_lo_made")
        keys_turned, keys_kept, gate_made, gate_kept = sems("keys_turned keys_kept gate_made gate_kept")
        x_turned, x_hi_made, x_lo_made, xv_made, x_kept = sems("x_turned x_hi_made x_lo_made xv_made x_kept")
        proj_made, proj_kept, biased = sems("proj_made proj_kept biased")
        qk_turned, v_turned, k_placed, v_placed = sems("qk_turned v_turned k_placed v_placed")
        scores_made, max_made, shifted, exp_made, probs_turned = sems(
            "scores_made max_made shifted exp_made probs_turned")
        ctx_made, ctx_turned, inv_made, attn_made, pre1_made, x1_made = sems(
            "ctx_made ctx_turned inv_made attn_made pre1_made x1_made")
        x1_turned, x1_hi_made, x1_lo_made = sems("x1_turned x1_hi_made x1_lo_made")
        gscore_made, gmax_made, gbias_made, gexp_made, ginv_made, coef_made = sems(
            "gscore_made gmax_made gbias_made gexp_made ginv_made coef_made")
        h_made, h_hi_made, h_lo_made = sems("h_made h_hi_made h_lo_made")
        x1_used, out_made, pre2_made, y_made, y_stored, y_free, last_stored = sems(
            "x1_used out_made pre2_made y_made y_stored y_free last_stored")
        moments_made = sems("moments_made1 moments_made2")
        eps_added = sems("eps_added1 eps_added2")
        rstd_made = sems("rstd_made1 rstd_made2")

        block = ctx.enter_context(nc.Block())

        @block.sync
        def _(sp):
            def place_k(u, scores_read, turned):
                sp.wait_ge(qk_turned, turned)
                wait_if_any(sp, scores_made, scores_read)
                for r in range(NQ):
                    sp.dma_start(k_diag[Q * r:Q * r + HD, r, :, :], k_T[Q * r:Q * r + HD, u, :, :])\
                        .then_inc(k_placed, 16)

            def place_v(u, context_read, turned):
                sp.wait_ge(v_turned, turned)
                wait_if_any(sp, ctx_made, context_read)
                for c in range(NQ):
                    sp.dma_start(v_diag[Q * c:Q * c + Q, c, 0:HD, :], v_T[Q * c:Q * c + Q, u, :, :])\
                        .then_inc(v_placed, 16)

            def load_x(b):
                wait_if_any(sp, x_turned, at(b, U, 0))
                wait_if_any(sp, x_kept, b)
                sp.dma_start(x_in[:], x[b].rearrange("(u p) i -> p u i", p=P)).then_inc(x_loaded, 16)

            for c in range(C):
                cols = slice(c * P, (c + 1) * P)
                sp.dma_start(w_raw[0][:, :, cols], wq[:, cols].rearrange("(c p) i -> p c i", p=P))\
                    .then_inc(wq_loaded[c], 16)
            load_x(0)
            sp.dma_start(w_raw[1], wk.rearrange("(c p) i -> p c i", p=P)).then_inc(w_loaded[1], 16)
            sp.dma_start(w_raw[2], wv.rearrange("(c p) i -> p c i", p=P)).then_inc(w_loaded[2], 16)
            load_x(1)
            sp.wait_ge(k_diag_zero, 1)
            place_k(0, 0, 2)
            place_k(1, 1, 4)
            sp.wait_ge(v_diag_zero, 1)
            place_v(0, 0, 1)
            with sp.Fori(1, B - 1) as b:
                tiles_before, tile_after = (sp.to_reg(at(b, U, k)) for k in range(2))
                last_tile = sp.to_reg(at(b - 1, U, 1))
                first_qk, all_qk = (sp.to_reg(at(b, 2 * U, k)) for k in (2, 4))
                turned, kept = sp.to_reg(at(b + 1, U, 0)), sp.to_reg(b + 1)
                place_v(1, last_tile, tiles_before)
                place_k(0, tiles_before, first_qk)
                place_k(1, tile_after, all_qk)
                sp.wait_ge(x_turned, turned)
                sp.wait_ge(x_kept, kept)
                sp.dma_start(x_in[:], x[b + 1].rearrange("(u p) i -> p u i", p=P)).then_inc(x_loaded, 16)
                place_v(0, tiles_before, tile_after)
            place_v(1, at(B - 2, U, 1), at(B - 1, U, 0))
            place_k(0, at(B - 1, U, 0), at(B - 1, 2 * U, 2))
            place_k(1, at(B - 1, U, 1), at(B - 1, 2 * U, 4))
            place_v(0, at(B - 1, U, 0), at(B - 1, U, 1))
            place_v(1, at(B - 1, U, 1), at(B - 1, U, 2))
            for u in range(U):
                sp.wait_ge(y_made, at(B - 1, U, u + 1))
                sp.dma_start(out[B - 1, u * P:(u + 1) * P], y[:, u, :]).then_inc(last_stored, 16)
            sp.wait_ge(last_stored, 16 * U)

        @block.gpsimd
        def _(pool):
            def store_y(b):
                for u in range(U):
                    pool.wait_ge(y_made, at(b, U, u + 1))
                    pool.dma_start(out[b, u * P:(u + 1) * P], y[:, u, :]).then_inc(y_stored, 16)

            def free_y(b):
                pool.wait_ge(y_stored, at(b, 16 * U, 16 * U))
                pool.sem_inc(y_free, 1)

            def inverse_deviation(b, u, n):
                pool.wait_ge(moments_made[n], at(b, U, u + 1))
                nc.gpsimd.tensor_tensor(var_eps[:, n, u:u + 1], moments[:, n, u, 1:2], eps[:], ALU.add)\
                    .then_inc(eps_added[n], 1)
                pool.wait_ge(eps_added[n], at(b, U, u + 1))
                nc.gpsimd.tensor_tensor(rstd[:, n, u:u + 1], var_eps[:, n, u:u + 1], minus_half[:], ALU.pow)\
                    .then_inc(rstd_made[n], 1)

            def add_bias_qk(b, u):
                for w in range(2):
                    pool.wait_ge(proj_kept, at(b, 3 * U, 2 * u + w + 1))
                    nc.gpsimd.tensor_tensor(qk_tok[:, w, u, 0:D], qk_tok[:, w, u, 0:D], bias[:, w, :], ALU.add)\
                        .then_inc(biased, 1)

            def add_bias_v(b, u):
                pool.wait_ge(proj_kept, at(b, 3 * U, 2 * U + u + 1))
                nc.gpsimd.tensor_tensor(v_tok[:, u, :], v_tok[:, u, :], bias[:, 2, :], ALU.add).then_inc(biased, 1)

            def step(b):
                add_bias_qk(b, 0)
                inverse_deviation(b - 1, 0, 0)
                add_bias_qk(b, 1)
                add_bias_v(b, 0)
                inverse_deviation(b - 1, 1, 0)
                add_bias_v(b, 1)

            pool.sem_inc(y_free, 1)
            nc.gpsimd.memset(ident[:], 0.0).then_inc(consts_set, 1)
            nc.gpsimd.memset(minus_half[:], -0.5).then_inc(consts_set, 1)
            nc.gpsimd.memset(eps[:], LN_EPS).then_inc(consts_set, 1)
            pool.wait_ge(consts_set, 3)
            nc.gpsimd.affine_select(out=ident[:], in_=ident[:], compare_op=ALU.not_equal, fill=1.0, base=0,
                                    pattern=[[-1, P]], channel_multiplier=1).then_inc(ident_ready, 1)
            nc.gpsimd.memset(qk_tok[:, :, :, D:], 0.0).then_inc(pads_ready, 1)
            pool.wait_ge(w_turned, 2 * C)
            nc.gpsimd.memset(k_diag[:], 0.0).then_inc(k_diag_zero, 1)
            pool.wait_ge(bias_loaded, 3 * 16)
            add_bias_qk(0, 0)
            add_bias_qk(0, 1)
            pool.wait_ge(w_turned, 3 * C)
            nc.gpsimd.memset(v_diag[:], 0.0).then_inc(v_diag_zero, 1)
            for u in range(U):
                add_bias_v(0, u)
            with pool.Fori(1, B - 1) as b:
                step(b)
                for u in range(U):
                    inverse_deviation(b - 1, u, 1)
                store_y(b - 1)
                free_y(b - 1)
            step(B - 1)
            for u in range(U):
                inverse_deviation(B - 1, u, 0)
            for u in range(U):
                inverse_deviation(B - 2, u, 1)
            store_y(B - 2)
            free_y(B - 2)
            for u in range(U):
                inverse_deviation(B - 1, u, 1)

        @block.scalar
        def _(act):
            def weight_high(n):
                act.wait_ge(w_turned, n + 1)
                nc.scalar.copy(w_hi[:, n // C, n % C, :], weight_bank(n)).then_inc(w_hi_made, 1)

            def x_high(b, x1_done=None):
                for u in range(U):
                    act.wait_ge(x_turned, at(b, U, u + 1))
                    if u and x1_done is not None:
                        act.wait_ge(x1_used, x1_done)
                    nc.scalar.copy(feat_hi[:, :, u * P:(u + 1) * P],
                                   ps_turn[:, u, :].rearrange("p (c t) -> p c t", c=C)).then_inc(x_hi_made, 1)

            def x_for_v(b, outputs_done=None):
                if outputs_done is not None:
                    act.wait_ge(out_made, outputs_done)
                for made, source, target in ((x_hi_made, feat_hi, xv_hi), (x_lo_made, feat_lo, xv_lo)):
                    for u in range(U):
                        act.wait_ge(made, at(b, U, u + 1))
                        nc.scalar.copy(target[:, u].rearrange("p c (k m) -> p c k m", k=NQ),
                                       source[:, :, u * P:(u + 1) * P].bitcast(F32)
                                       .rearrange("p c (m k) -> p c k m", k=NQ)).then_inc(xv_made, 1)

            def keep_x(b):
                wait_if_any(act, x1_made, at(b, U, 0))
                act.wait_ge(x_loaded, at(b, 16, 16))
                nc.scalar.copy(pre1, x_in[:]).then_inc(x_kept, 1)

            def keep_qk(b, u, projections=(0, 1)):
                wait_if_any(act, qk_turned, at(b - 1, 2 * U, 2 * u + 2) if not isinstance(b, int) or b else 0)
                for w in projections:
                    act.wait_ge(proj_made, at(b, 3 * U, 2 * u + w + 1))
                    nc.scalar.copy(qk_tok[:, w, u, 0:D], ps_lin[:, w, :]).then_inc(proj_kept, 1)

            def keep_v(b):
                wait_if_any(act, y_free, b)
                for u in range(U):
                    act.wait_ge(proj_made, at(b, 3 * U, 2 * U + u + 1))
                    nc.scalar.copy(v_tok[:, u, :], ps_lin[:, u, :]).then_inc(proj_kept, 1)

            def x1_high(b):
                for c in range(C):
                    act.wait_ge(x1_turned, at(b, 2, c // 2 + 1))
                    nc.scalar.activation(feat_hi[:, c, :], ps_turn[:, c // 2, c % 2 * S:(c % 2 + 1) * S], ACT.Copy,
                                         accum_out=x1_sum[:, c:c + 1]).then_inc(x1_hi_made, 1)

            def gate_exp(b, bank=1):
                act.wait_ge(gbias_made, b + 1)
                nc.scalar.activation(gexp[:], ps_lin[:, bank, 0:E], ACT.Exp, bias=gbias[:], scale=GATE_SCALE,
                                     accum_out=gsum[:]).then_inc(gexp_made, 1)

            def exponentials(b, u):
                act.wait_ge(shifted, at(b, U, u + 1))
                nc.scalar.activation(probs[:, u], probs[:, u], ACT.Exp, scale=SCORE_SCALE).then_inc(exp_made, 1)

            def h_high(b, fill=None):
                act.wait_ge(coef_made, at(b, EPC, EPC))
                for m in range(M):
                    if m == M // 2 and fill:
                        fill()
                    act.wait_ge(h_made, at(b, M // 2, m // 2 + 1))
                    nc.scalar.mul(h_hi[:, m, :], ps_turn[:, m // 2, m % 2 * S:(m % 2 + 1) * S],
                                  coef[:, m:m + 1]).then_inc(h_hi_made, 1)

            def load_up(half):
                wait_if_any(act, up_lo_made, half)
                rows = slice(half * MU, (half + 1) * MU)
                act.dma_start(up_raw, lora_up.rearrange("e r o -> (e r) o").rearrange("(m p) o -> p m o", p=P)[:, rows])\
                    .then_inc(up_loaded, 16)

            def up_high(half):
                act.wait_ge(up_loaded, 16 * (half + 1))
                nc.scalar.copy(up_hi[:, half * MU:(half + 1) * MU, :], up_raw).then_inc(up_hi_made, 1)

            def step(b):
                keep_qk(b, 0)
                keep_qk(b, 1)
                keep_v(b)
                keep_x(b)
                x1_high(b - 1)
                exponentials(b, 0)
                gate_exp(b - 1)
                h_high(b - 1, fill=lambda: exponentials(b, 1))

            for n, v in enumerate((bq, bk, bv)):
                act.dma_start(bias[:, n, :], v.partition_broadcast(P)).then_inc(bias_loaded, 16)
            for n in range(C):
                weight_high(n)
            x_high(0)
            for c in range(C):
                act.dma_start(down_raw[:, c, :].rearrange("p (e r) -> p e r", e=E),
                              lora_down[:, c * P:(c + 1) * P, :].rearrange("e p r -> p e r")).then_inc(down_loaded, 16)
            keep_x(0)
            for n in range(C, 2 * C):
                weight_high(n)
            act.dma_start(keys[:], lora_keys).then_inc(gate_loaded, 16)
            act.dma_start(gate_raw[:], w_gate).then_inc(gate_loaded, 16)
            x_for_v(0)
            act.wait_ge(pads_ready, 1)
            keep_qk(0, 0, (0,))
            for n in range(2 * C, 3 * C):
                weight_high(n)
            act.dma_start(w_raw[3], w_org.rearrange("(c p) i -> p c i", p=P)).then_inc(w_loaded[3], 16)
            load_up(0)
            keep_qk(0, 0, (1,))
            keep_qk(0, 1)
            act.wait_ge(down_loaded, 16 * C)
            nc.scalar.copy(down_hi[:], down_raw).then_inc(down_hi_made, 1)
            keep_v(0)
            for n in range(3 * C, 4 * C):
                weight_high(n)
            exponentials(0, 0)
            x_high(1)
            up_high(0)
            x_for_v(1)
            load_up(1)
            exponentials(0, 1)
            up_high(1)
            with act.Fori(1, B - 1) as b:
                step(b)
                x_high(b + 1, x1_done=b)
                x_for_v(b + 1, outputs_done=at(b, U, 0))
            step(B - 1)
            x1_high(B - 1)
            gate_exp(B - 1, 0)
            h_high(B - 1)

        @block.vector
        def _(dve):
            def weight_low(n):
                dve.wait_ge(w_hi_made, n + 1)
                nc.vector.tensor_tensor(w_lo[:, n // C, n % C, :], weight_bank(n),
                                        w_hi[:, n // C, n % C, :].bitcast(F32), ALU.subtract).then_inc(w_lo_made, 1)

            def x_low(b, u):
                dve.wait_ge(x_hi_made, at(b, U, u + 1))
                nc.vector.tensor_tensor(feat_lo[:, :, u * P:(u + 1) * P],
                                        ps_turn[:, u, :].rearrange("p (c t) -> p c t", c=C),
                                        feat_hi[:, :, u * P:(u + 1) * P].bitcast(F32),
                                        ALU.subtract).then_inc(x_lo_made, 1)

            def turn_qk(b, u, first=False):
                if not first:
                    dve.wait_ge(scores_made, at(b - 1, U, u + 1))
                    dve.wait_ge(k_placed, at(b - 1, NQ * 16 * U, NQ * 16 * (u + 1)))
                for w, turned in enumerate((q_T, k_T)):
                    dve.wait_ge(biased, at(b, 3 * U, 2 * u + w + 1))
                    heads = qk_tok[:, w, u, :]
                    squares = bass.AP(tensor=heads.tensor, offset=heads.offset, ap=[heads.ap[0], [HD, H], [1, Q]])
                    nc.vector.transpose(turned[:, u].rearrange("p j h -> p h j"), squares).then_inc(qk_turned, 1)

            def turn_v(b, u, first=False):
                if not first:
                    dve.wait_ge(v_placed, at(b - 1, NQ * 16 * U, NQ * 16 * (u + 1)))
                dve.wait_ge(biased, at(b, 3 * U, 2 * U + u + 1))
                nc.vector.transpose(v_T[:, u], v_tok[:, u, :].rearrange("p (t d) -> p d t", d=HD))\
                    .then_inc(v_turned, 1)

            def shift_scores(b, u):
                scores = ps_att[:, u].rearrange("p a (m t) -> p (a m) t", t=H)
                dve.wait_ge(scores_made, at(b, U, u + 1))
                nc.vector.reduce_max(row_max[:, u, :], scores, AX_X).then_inc(max_made, 1)
                dve.wait_ge(max_made, at(b, U, u + 1))
                nc.vector.tensor_tensor(probs[:, u], scores, row_max[:, u, :].unsqueeze(2).to_broadcast([P, J, H]),
                                        ALU.subtract).then_inc(shifted, 1)

            def turn_probs(b, u):
                dve.wait_ge(exp_made, at(b, U, u + 1))
                nc.vector.transpose(probs_T[:, u], probs[:, u]).then_inc(probs_turned, 1)

            def moments_of(u, n, source):
                nc.vector.bn_stats(stats[:, n, u, :], source[:, u, :])
                dve.drain()
                nc.vector.bn_aggr(moments[:, n, u, :], stats[:, n, u, :]).then_inc(moments_made[n], 1)

            def normalise(b, u, n, target, source, made):
                dve.wait_ge(rstd_made[n], at(b, U, u + 1))
                nc.vector.tensor_scalar(target[:, u, :], source[:, u, :], moments[:, n, u, 0:1],
                                        rstd[:, n, u:u + 1], ALU.subtract, ALU.mult).then_inc(made, 1)

            def add_attention(b, u):
                dve.wait_ge(ctx_made, at(b, U, u + 1))
                source = ps_att[:, u, :, 0:HALF * NQ * DA].rearrange("p a (j d) -> p d a j", d=DA)
                nc.vector.transpose(ctx_tok[u], source).then_inc(ctx_turned, 1)
                dve.wait_ge(ctx_turned, at(b, U, u + 1))
                nc.vector.reciprocal(inv_sum[:, u, :], ctx_tok[u][:, HD, :]).then_inc(inv_made, 1)
                dve.wait_ge(inv_made, at(b, U, u + 1))
                nc.vector.tensor_tensor(ctx_tok[u][:, 0:HD, :], ctx_tok[u][:, 0:HD, :],
                                        inv_sum[:, u, :].unsqueeze(1).to_broadcast([P, HD, H]),
                                        ALU.mult).then_inc(attn_made, 1)
                dve.wait_ge(attn_made, at(b, U, u + 1))
                dve.wait_ge(x_kept, b + 1)
                by_feature = pre1[:, u, :].rearrange("p (h d) -> p d h", h=H)
                nc.vector.tensor_tensor(by_feature, by_feature, ctx_tok[u][:, 0:HD, :], ALU.add)\
                    .then_inc(pre1_made, 1)
                dve.wait_ge(pre1_made, at(b, U, u + 1))
                moments_of(u, 0, pre1)

            def x1_low(b):
                for k in range(C // 2):
                    dve.wait_ge(x1_hi_made, at(b, C, 2 * k + 2))
                    chunks = slice(2 * k, 2 * k + 2)
                    nc.vector.tensor_tensor(feat_lo[:, chunks, :], ps_turn[:, k, :].rearrange("p (c t) -> p c t", c=2),
                                            feat_hi[:, chunks, :].bitcast(F32), ALU.subtract).then_inc(x1_lo_made, 1)

            def gate_shift(b, bank=1):
                dve.wait_ge(gscore_made, b + 1)
                nc.vector.reduce_max(gmax[:], ps_lin[:, bank, 0:E], AX_X).then_inc(gmax_made, 1)
                dve.wait_ge(gmax_made, b + 1)
                nc.vector.tensor_scalar(gbias[:], gmax[:], -GATE_SCALE, None, ALU.mult).then_inc(gbias_made, 1)

            def gate_coefficients(b):
                dve.wait_ge(gexp_made, b + 1)
                nc.vector.reciprocal(ginv[:], gsum[:]).then_inc(ginv_made, 1)
                dve.wait_ge(ginv_made, b + 1)
                for e in range(EPC):
                    rows = slice(R * e, R * (e + 1))
                    nc.vector.tensor_scalar(coef[rows, :], gexp[rows, e:E:EPC], ginv[rows, :], None, ALU.mult)\
                        .then_inc(coef_made, 1)

            def h_low(b, half):
                for m in range(M // 2 * half, M // 2 * (half + 1)):
                    dve.wait_ge(h_hi_made, at(b, M, m // 2 * 2 + 2))
                    nc.vector.scalar_tensor_tensor(h_lo[:, m, :], ps_turn[:, m // 2, m % 2 * S:(m % 2 + 1) * S],
                                                   coef[:, m:m + 1], h_hi[:, m, :].bitcast(F32),
                                                   ALU.mult, ALU.subtract).then_inc(h_lo_made, 1)

            def add_outputs(b, u, x1=x1):
                dve.wait_ge(out_made, at(b, U, u + 1))
                nc.vector.tensor_tensor(pre2[:, u, :], ps_lin[:, u, :], x1[:, u, :], ALU.add).then_inc(pre2_made, 1)
                dve.wait_ge(pre2_made, at(b, U, U + u + 1))
                moments_of(u, 1, pre2)

            def up_low(half):
                dve.wait_ge(up_hi_made, half + 1)
                rows = slice(half * MU, (half + 1) * MU)
                nc.vector.tensor_tensor(up_lo[:, rows, :], up_raw, up_hi[:, rows, :].bitcast(F32), ALU.subtract)\
                    .then_inc(up_lo_made, 1)

            def step(b):
                turn_qk(b, 0)
                add_attention(b - 1, 0)
                normalise(b - 1, 0, 0, x1, pre1, x1_made)
                turn_qk(b, 1)
                add_attention(b - 1, 1)
                turn_v(b, 0)
                normalise(b - 1, 1, 0, x1, pre1, x1_made)
                shift_scores(b, 0)
                x1_low(b - 1)
                turn_v(b, 1)
                turn_probs(b, 0)
                gate_shift(b - 1)
                gate_coefficients(b - 1)
                shift_scores(b, 1)
                h_low(b - 1, 0)
                turn_probs(b, 1)
                h_low(b - 1, 1)

            dve.sem_inc(pre2_made, U)
            for n in range(C):
                weight_low(n)
            for u in range(U):
                x_low(0, u)
            for n in range(C, 2 * C):
                weight_low(n)
            for n in range(2 * C, 3 * C):
                weight_low(n)
            turn_qk(0, 0, first=True)
            dve.wait_ge(keys_turned, 1)
            nc.vector.tensor_copy(keys_T[:], ps_turn[:, 0, 0:E]).then_inc(keys_kept, 1)
            turn_qk(0, 1, first=True)
            dve.wait_ge(gate_made, 1)
            nc.vector.tensor_copy(gate[:], ps_turn[:, 1, 0:C * E].rearrange("p (c e) -> p c e", c=C))\
                .then_inc(gate_kept, 1)
            dve.wait_ge(down_hi_made, 1)
            nc.vector.tensor_tensor(down_lo[:], down_raw, down_hi[:].bitcast(F32), ALU.subtract)\
                .then_inc(down_lo_made, 1)
            dve.wait_ge(v_diag_zero, 1)
            for c in range(NQ):
                nc.vector.memset(v_diag[Q * c:Q * c + Q, c, HD, :], 1.0).then_inc(ones_placed, 1)
            turn_v(0, 0, first=True)
            shift_scores(0, 0)
            for n in range(3 * C, 4 * C):
                weight_low(n)
            turn_v(0, 1, first=True)
            for u in range(U):
                x_low(1, u)
            turn_probs(0, 0)
            shift_scores(0, 1)
            up_low(0)
            turn_probs(0, 1)
            up_low(1)
            with dve.Fori(1, B - 1) as b:
                step(b)
                add_outputs(b - 1, 0)
                x_low(b + 1, 0)
                normalise(b - 1, 0, 1, y, pre2, y_made)
                x_low(b + 1, 1)
                add_outputs(b - 1, 1)
                normalise(b - 1, 1, 1, y, pre2, y_made)
            step(B - 1)
            for u in range(U):
                add_attention(B - 1, u)
            for u in range(U):
                normalise(B - 1, u, 0, pre1, pre1, x1_made)
            add_outputs(B - 2, 0)
            normalise(B - 2, 0, 1, y, pre2, y_made)
            x1_low(B - 1)
            add_outputs(B - 2, 1)
            normalise(B - 2, 1, 1, y, pre2, y_made)
            gate_shift(B - 1, 0)
            gate_coefficients(B - 1)
            for half in range(2):
                h_low(B - 1, half)
            dve.wait_ge(y_free, B)
            add_outputs(B - 1, 0, pre1)
            normalise(B - 1, 0, 1, y, pre2, y_made)
            add_outputs(B - 1, 1, pre1)
            normalise(B - 1, 1, 1, y, pre2, y_made)

        @block.tensor
        def _(pe):
            def product(out, left, right, first, last):
                nc.tensor.matmul(out, left[0], right[0], start=first, stop=False)
                nc.tensor.matmul(out, left[0], right[1], start=False, stop=False)
                return nc.tensor.matmul(out, left[1], right[0], start=False, stop=last)

            def turn_weight(w):
                if w:
                    pe.wait_ge(w_loaded[w], 16)
                for c in range(C):
                    n = w * C + c
                    if w == 0:
                        pe.wait_ge(wq_loaded[c], 16)
                    wait_if_any(pe, w_lo_made, n - WEIGHT_BANKS[w] + 1)
                    for o in range(C):
                        ins = nc.tensor.transpose(weight_bank(n)[:, o * P:(o + 1) * P],
                                                  w_raw[w][:, o, c * P:(c + 1) * P], ident[:])
                    ins.then_inc(w_turned, 1)

            def turn_x(b):
                pe.wait_ge(x_loaded, at(b, 16, 16))
                for u in range(U):
                    for c in range(C):
                        ins = nc.tensor.transpose(ps_turn[:, u, c * P:(c + 1) * P], x_in[:, u, c * P:(c + 1) * P],
                                                  ident[:])
                    ins.then_inc(x_turned, 1)

            def project_qk(b, u, w):
                pe.wait_ge(x_lo_made, at(b, U, u + 1))
                if u:
                    pe.wait_ge(proj_kept, at(b, 3 * U, 2 * u + w - 1))
                elif not isinstance(b, int) or b:
                    pe.wait_ge(pre2_made, at(b - 1, U, w + 1))
                for c in range(C):
                    cols = slice(u * P, (u + 1) * P)
                    ins = product(ps_lin[:, w, :], (feat_hi[:, c, cols], feat_lo[:, c, cols]),
                                  (w_hi[:, w, c, :], w_lo[:, w, c, :]), c == 0, c == C - 1)
                ins.then_inc(proj_made, 1)

            def project_v(b, u):
                pe.wait_ge(xv_made, at(b, 2 * U, U + u + 1))
                pe.wait_ge(proj_kept, at(b, 3 * U, 2 * U + u - 1))
                for c in range(C):
                    ins = product(ps_lin[:, u, :], (xv_hi[:, u, c, :], xv_lo[:, u, c, :]),
                                  (w_hi[:, 2, c, :], w_lo[:, 2, c, :]), c == 0, c == C - 1)
                ins.then_inc(proj_made, 1)

            def scores(b, u, first=False):
                if not first:
                    pe.wait_ge(ctx_turned, at(b - 1, U, u + 1))
                pe.wait_ge(k_placed, at(b, NQ * 16 * U, NQ * 16 * (u + 1)))
                for g in range(G):
                    for c in range(NQ):
                        j = NQ * g + c
                        cols = slice(g % HALF * P, (g % HALF + 1) * P)
                        ins = nc.tensor.matmul(ps_att[Q * c:Q * c + Q, u, g // HALF, cols]
                                               .rearrange("h (r t) -> h r t", r=NQ),
                                               q_T[:, u, j, :], k_diag[:, :, j, :], start=True, stop=True)
                ins.then_inc(scores_made, 1)

            def context(b, u):
                pe.wait_ge(v_placed, at(b, NQ * 16 * U, NQ * 16 * (u + 1)))
                pe.wait_ge(probs_turned, at(b, U, u + 1))
                for g in range(G):
                    for r in range(NQ):
                        cols = slice(g % HALF * NQ * DA, (g % HALF + 1) * NQ * DA)
                        ins = nc.tensor.matmul(ps_att[Q * r:Q * r + Q, u, g // HALF, cols]
                                               .rearrange("h (c d) -> h c d", c=NQ),
                                               probs_T[:, u, NQ * g + r, :], v_diag[:, :, :, G * r + g],
                                               start=True, stop=True)
                ins.then_inc(ctx_made, 1)

            def turn_x1(b, x1):
                pe.wait_ge(x1_made, at(b, U, U))
                for c in range(C):
                    for u in range(U):
                        place = c % 2 * S + u * P
                        ins = nc.tensor.transpose(ps_turn[:, c // 2, place:place + P], x1[:, u, c * P:(c + 1) * P],
                                                  ident[:])
                    if c % 2:
                        ins.then_inc(x1_turned, 1)

            def gate_scores(b, bank):
                pe.wait_ge(x1_hi_made, at(b, C, C))
                for r in range(NQ):
                    for c in range(C):
                        ins = nc.tensor.matmul(ps_lin[Q * r:Q * r + Q, bank, 0:E],
                                               x1_sum[:, c:c + 1].to_broadcast([P, Q]),
                                               gate[:, c, :], start=(c == 0), stop=(c == C - 1))
                ins.then_inc(gscore_made, 1)

            def hidden(b):
                pe.wait_ge(x1_lo_made, at(b, C // 2, C // 2))
                for m in range(M):
                    rows = slice(m * P, (m + 1) * P)
                    for c in range(C):
                        ins = product(ps_turn[:, m // 2, m % 2 * S:(m % 2 + 1) * S],
                                      (down_hi[:, c, rows], down_lo[:, c, rows]), (feat_hi[:, c, :], feat_lo[:, c, :]),
                                      c == 0, c == C - 1)
                    if m % 2:
                        ins.then_inc(h_made, 1)

            def outputs(b, u, between=None):
                cols = slice(u * P, (u + 1) * P)
                for c in range(C):
                    ins = product(ps_lin[:, u, :], (feat_hi[:, c, cols], feat_lo[:, c, cols]),
                                  (w_hi[:, 3, c, :], w_lo[:, 3, c, :]), c == 0, False)
                if u:
                    ins.then_inc(x1_used, 1)
                if between:
                    between()
                for m in range(M):
                    if u == 0:
                        pe.wait_ge(h_lo_made, at(b, M, m + 1))
                    ins = product(ps_lin[:, u, :], (h_hi[:, m, cols], h_lo[:, m, cols]),
                                  (up_hi[:, m, :], up_lo[:, m, :]), False, m == M - 1)
                ins.then_inc(out_made, 1)

            def step(b):
                for w in range(2):
                    project_qk(b, 0, w)
                context(b - 1, 0)
                for w in range(2):
                    project_qk(b, 1, w)
                context(b - 1, 1)
                scores(b, 0)
                for u in range(U):
                    project_v(b, u)
                turn_x1(b - 1, x1)
                scores(b, 1)
                pe.wait_ge(proj_kept, at(b, 3 * U, 3 * U))
                gate_scores(b - 1, 1)
                hidden(b - 1)
                pe.wait_ge(gexp_made, b)

            pe.wait_ge(ident_ready, 1)
            turn_weight(0)
            turn_x(0)
            turn_weight(1)
            pe.wait_ge(w_lo_made, C)
            project_qk(0, 0, 0)
            turn_weight(2)
            pe.wait_ge(w_lo_made, 2 * C)
            project_qk(0, 0, 1)
            pe.wait_ge(gate_loaded, 2 * 16)
            nc.tensor.transpose(ps_turn[:, 0, 0:E], keys[:], ident[0:E, 0:E]).then_inc(keys_turned, 1)
            project_qk(0, 1, 0)
            pe.wait_ge(keys_kept, 1)
            for c in range(C):
                ins = nc.tensor.matmul(ps_turn[:, 1, c * E:(c + 1) * E], gate_raw[:, c * P:(c + 1) * P], keys_T[:],
                                       start=True, stop=True)
            ins.then_inc(gate_made, 1)
            project_qk(0, 1, 1)
            pe.wait_ge(w_lo_made, 3 * C)
            project_v(0, 0)
            scores(0, 0, first=True)
            project_v(0, 1)
            turn_weight(3)
            pe.wait_ge(gate_kept, 1)
            turn_x(1)
            pe.wait_ge(w_lo_made, 4 * C)
            scores(0, 1, first=True)
            pe.wait_ge(down_lo_made, 1)
            pe.wait_ge(ones_placed, NQ)
            with pe.Fori(1, B - 1) as b:
                step(b)
                outputs(b - 1, 0)
                turn_x(b + 1)
                outputs(b - 1, 1)
            step(B - 1)
            for u in range(U):
                context(B - 1, u)
            outputs(B - 2, 0)
            outputs(B - 2, 1, between=lambda: turn_x1(B - 1, pre1))
            pe.wait_ge(pre2_made, at(B - 1, U, 1))
            gate_scores(B - 1, 0)
            hidden(B - 1)
            pe.wait_ge(gexp_made, B)
            outputs(B - 1, 0)
            pe.wait_ge(pre2_made, at(B - 1, U, 2))
            outputs(B - 1, 1)


_INS = ['L0_attn_hidden_states', 'L0_attn_wq', 'L0_attn_bq', 'L0_attn_wk', 'L0_attn_bk', 'L0_attn_wv', 'L0_attn_bv',
        'L0_ffn_W_org', 'L0_ffn_lora_down', 'L0_ffn_lora_up', 'L0_ffn_lora_keys', 'L0_ffn_Wq']


def kernel(**inputs):
    import numpy as _np
    import concourse.bacc as _bacc
    from concourse import mybir as _mybir
    from concourse.bass_utils import run_bass_kernel_spmd as _run

    nc = _bacc.Bacc("TRN2", target_bir_lowering=False, num_devices=1)
    arrays, args = {}, []
    for name in _INS:
        a = _np.ascontiguousarray(inputs[name])
        arrays[f"in_{name}_dram"] = a
        args.append(nc.dram_tensor(f"in_{name}_dram", a.shape, _mybir.dt.from_np(a.dtype), kind="ExternalInput").ap())
    shape = inputs['L0_attn_hidden_states'].shape
    args.append(nc.dram_tensor("out_0_dram", shape, _mybir.dt.float32, kind="ExternalOutput").ap())
    seq_postln_kernel(nc, *args)
    r = _run(nc, [arrays], core_ids=[0])
    return r.results[0]["out_0_dram"]
```

```python
from contextlib import ExitStack

import concourse.bass as bass
from concourse import mybir

ALU = mybir.AluOpType
ACT = mybir.ActivationFunctionType
F32 = mybir.dt.float32
F32R = mybir.dt.float32r
AX_X = mybir.AxisListType.X

P = 128
Q = 32
NQ = P // Q
LN_EPS = 1e-5


def wait_if_any(engine, semaphore, value):
    if not isinstance(value, int) or value > 0:
        engine.wait_ge(semaphore, value)


def at(b, per_batch, k):
    return b * per_batch + k


def qk_place(b, u, w):
    return w * 2 + u + 1 if isinstance(b, int) and b == 0 else u * 2 + w + 1


def seq_postln_kernel(nc, x, wq, bq, wk, bk, wv, bv, w_org, lora_down, lora_up, lora_keys, w_gate, out):
    B, S, D = x.shape
    E, _, R = lora_down.shape
    KD = lora_keys.shape[1]
    C = D // P
    U = S // P
    H = Q
    HD = D // H
    DA = HD + 1
    J = Q
    G = J // NQ
    HALF = G // 2
    M = E * R // P
    EPC = P // R
    assert D == 512 and H * HD == D and U == 2 and KD == P and E * R == D and EPC == 2
    SCORE_SCALE = float(HD) ** -0.5
    GATE_SCALE = 1.0 / (S * float(KD) ** 0.5)

    ctx = ExitStack()
    with ctx:
        def sb(name, shape, dtype=F32):
            return ctx.enter_context(nc.sbuf_tensor(name, shape, dtype))

        def flat(tensor):
            names = "abcd"[:len(tensor.shape) - 1]
            return tensor[:].rearrange(f"p {' '.join(names)} -> p ({' '.join(names)})")

        def psum(name, shape):
            return ctx.enter_context(nc.psum_tensor(name, shape, F32))

        def sem(name):
            return ctx.enter_context(nc.semaphore(name))

        ident = sb("ident", [P, P])
        minus_half = sb("minus_half", [P, 1])
        eps = sb("eps", [P, 1])
        w_hi = sb("w_hi", [P, 4, C, D], F32R)
        w_lo = sb("w_lo", [P, 4, C, D], F32R)
        down_hi = sb("down_hi", [P, C, E * R], F32R)
        down_lo = sb("down_lo", [P, C, E * R], F32R)
        up_hi = sb("up_hi", [P, M, D], F32R)
        up_lo = sb("up_lo", [P, M, D], F32R)
        bias = sb("bias", [P, 3, D])
        keys = sb("keys", [E, KD])
        keys_T = sb("keys_T", [KD, E])
        gate_raw = sb("gate_raw", [KD, D])
        gate = sb("gate", [P, C, E])

        x_in = sb("x_in", [P, U, D])
        feat_hi = sb("feat_hi", [P, C, S], F32R)
        feat_lo = sb("feat_lo", [P, C, S], F32R)
        aux_hi = sb("aux_hi", [P, C * S], F32R)
        aux_lo = sb("aux_lo", [P, C * S], F32R)
        xv_hi, xv_lo = (t[:].rearrange("p (u c t) -> p u c t", u=U, c=C) for t in (aux_hi, aux_lo))
        h_hi, h_lo = (t[:].rearrange("p (m t) -> p m t", m=M) for t in (aux_hi, aux_lo))
        qk_tok = sb("qk_tok", [P, 2, U, D + Q - HD])
        q_T = sb("q_T", [P, U, J, H])
        k_T = sb("k_T", [P, U, J, H])
        v_T = sb("v_T", [P, U, HD, J])
        k_diag = sb("k_diag", [P, NQ, J, H])
        v_diag = sb("v_diag", [P, NQ, DA, J])
        probs = sb("probs", [P, U, J, H])
        probs_T = sb("probs_T", [P, U, J, H])
        row_max = sb("row_max", [P, U, J])
        ctx_tok = [probs_T[:, u].rearrange("p j h -> p (j h)")[:, 0:DA * H].rearrange("p (d h) -> p d h", h=H)
                   for u in range(U)]
        inv_sum = sb("inv_sum", [P, U, H])
        resid = sb("resid", [P, 2, U, D])
        pre1, x1 = resid[:, 0], resid[:, 1]
        tok = sb("tok", [P, U, D])
        v_tok, pre2, y = tok, tok, tok
        x1_sum = sb("x1_sum", [P, C])
        gmax = sb("gmax", [P, 1])
        gbias = sb("gbias", [P, 1])
        gexp = sb("gexp", [P, E])
        gsum = sb("gsum", [P, 1])
        ginv = sb("ginv", [P, 1])
        coef = sb("coef", [P, M])
        stats = sb("stats", [P, 2, U, 6])
        moments = sb("moments", [P, 2, U, 2])
        var_eps = sb("var_eps", [P, 2, U])
        rstd = sb("rstd", [P, 2, U])
        w_raw = [t.rearrange("p (c i) -> p c i", c=C)
                 for t in (flat(probs), flat(probs_T), flat(v_diag)[:, 0:C * D], flat(resid))]
        down_raw, up_raw = w_raw[0], w_raw[1]

        ps_lin = psum("ps_lin", [P, 2, D])
        ps_att = psum("ps_att", [P, U, 2, 512])
        ps_turn = psum("ps_turn", [P, 2, 512])

        HALVES = (slice(0, D // 2), slice(D // 2, D))
        half_banks = (ps_lin[:, 1, 0:D // 2], ps_att[:, 0, 0, 0:D // 2])

        def weight_bank(n):
            return ps_att[:, n % 4 // 2, n % 2, :]

        def sems(names):
            return [sem(name) for name in names.split()]

        x_loaded, gate_loaded, down_loaded, up_loaded = sems(
            "x_loaded gate_loaded down_loaded up_loaded")
        x0_loaded, wq_first_loaded, wq_rest_loaded = sems("x0_loaded wq_first_loaded wq_rest_loaded")
        bias_loaded = [sem(f"bias_loaded{n}") for n in range(3)]
        w_loaded = [None] + [sem(f"w_loaded{n}") for n in range(1, 4)]
        consts_set, ident_ready, pads_ready, k_diag_zero, v_diag_zero, ones_placed = sems(
            "consts_set ident_ready pads_ready k_diag_zero v_diag_zero ones_placed")
        w_turned, w_hi_made, w_lo_made = sems("w_turned w_hi_made w_lo_made")
        down_hi_made, down_lo_made, up_hi_made, up_lo_made = sems("down_hi_made down_lo_made up_hi_made up_lo_made")
        keys_turned, keys_kept, gate_made, gate_kept = sems("keys_turned keys_kept gate_made gate_kept")
        x_turned, x_hi_made, x_lo_made, xv_made, x_kept = sems("x_turned x_hi_made x_lo_made xv_made x_kept")
        proj_made, proj_kept, biased = sems("proj_made proj_kept biased")
        qk_turned, v_turned, k_placed, v_placed = sems("qk_turned v_turned k_placed v_placed")
        scores_made, max_made, shifted, exp_made, probs_turned = sems(
            "scores_made max_made shifted exp_made probs_turned")
        ctx_made, ctx_turned, inv_made, attn_made, pre1_made, x1_made = sems(
            "ctx_made ctx_turned inv_made attn_made pre1_made x1_made")
        x1_turned, x1_hi_made, x1_lo_made = sems("x1_turned x1_hi_made x1_lo_made")
        gscore_made, gmax_made, gbias_made, gexp_made, ginv_made, coef_made = sems(
            "gscore_made gmax_made gbias_made gexp_made ginv_made coef_made")
        h_made, h_hi_made, h_lo_made = sems("h_made h_hi_made h_lo_made")
        x1_used, out_made, pre2_made, y_made, y_stored, y_free = sems(
            "x1_used out_made pre2_made y_made y_stored y_free")
        half_made, half_added, half_normalised, last_stored = sems(
            "half_made half_added half_normalised last_stored")
        moments_made = sems("moments_made1 moments_made2")
        eps_added = sems("eps_added1 eps_added2")
        rstd_made = sems("rstd_made1 rstd_made2")

        block = ctx.enter_context(nc.Block())

        @block.sync
        def _(sp):
            def place_k(u, scores_read, turned):
                sp.wait_ge(qk_turned, turned)
                wait_if_any(sp, scores_made, scores_read)
                for r in range(NQ):
                    sp.dma_start(k_diag[Q * r:Q * r + HD, r, :, :], k_T[Q * r:Q * r + HD, u, :, :])\
                        .then_inc(k_placed, 16)

            def place_v(u, context_read, turned, blocks=range(NQ)):
                sp.wait_ge(v_turned, turned)
                wait_if_any(sp, ctx_made, context_read)
                for c in blocks:
                    sp.dma_start(v_diag[Q * c:Q * c + Q, c, 0:HD, :], v_T[Q * c:Q * c + Q, u, :, :])\
                        .then_inc(v_placed, 16)

            def load_rows(target, weight, cols, loaded):
                sp.dma_start(target[:, :, cols], weight[:, cols].rearrange("(c p) i -> p c i", p=P))\
                    .then_inc(loaded, 16)

            sp.dma_start(x_in[:, 0, :], x[0, 0:P]).then_inc(x0_loaded, 16)
            load_rows(w_raw[0], wq, slice(0, D // 2), wq_first_loaded)
            load_rows(w_raw[0], wq, slice(D // 2, D), wq_rest_loaded)
            sp.dma_start(x_in[:, 1, :], x[0, P:]).then_inc(x_loaded, 16)
            load_rows(w_raw[1], wk, slice(0, D), w_loaded[1])
            for n, v in enumerate((bq, bk)):
                sp.dma_start(bias[:, n, :], v.partition_broadcast(P)).then_inc(bias_loaded[n], 16)
            load_rows(w_raw[2], wv, slice(0, D), w_loaded[2])
            sp.dma_start(bias[:, 2, :], bv.partition_broadcast(P)).then_inc(bias_loaded[2], 16)
            sp.dma_start(keys[:], lora_keys).then_inc(gate_loaded, 16)
            sp.dma_start(gate_raw[:], w_gate).then_inc(gate_loaded, 16)
            sp.wait_ge(w_turned, C)
            for c in range(C):
                sp.dma_start(down_raw[:, c, :].rearrange("p (e r) -> p e r", e=E),
                             lora_down[:, c * P:(c + 1) * P, :].rearrange("e p r -> p e r")).then_inc(down_loaded, 16)
            sp.wait_ge(k_diag_zero, 1)
            place_k(0, 0, qk_place(0, 0, 1))
            sp.wait_ge(x_turned, U)
            sp.wait_ge(x_kept, 1)
            sp.dma_start(x_in[:], x[1].rearrange("(u p) i -> p u i", p=P)).then_inc(x_loaded, 16)
            place_k(1, 1, qk_place(0, 1, 1))
            sp.wait_ge(v_diag_zero, 1)
            place_v(0, 0, 1)
            with sp.Fori(1, B - 1) as b:
                tiles_before, tile_after = (sp.to_reg(at(b, U, k)) for k in range(2))
                last_tile = sp.to_reg(at(b - 1, U, 1))
                first_qk, all_qk = (sp.to_reg(at(b, 2 * U, k)) for k in (2, 4))
                turned, kept = sp.to_reg(at(b + 1, U, 0)), sp.to_reg(b + 1)
                first_y, all_y = (sp.to_reg(at(b - 1, U, k)) for k in (1, 2))
                stored = sp.to_reg(at(b, 16 * U, 0))
                place_v(1, last_tile, tiles_before, range(NQ // 2))
                place_k(0, tiles_before, first_qk)
                place_k(1, tile_after, all_qk)
                sp.wait_ge(x_turned, turned)
                sp.wait_ge(x_kept, kept)
                sp.dma_start(x_in[:], x[b + 1].rearrange("(u p) i -> p u i", p=P)).then_inc(x_loaded, 16)
                place_v(0, tiles_before, tile_after)
                for u in range(U):
                    sp.wait_ge(y_made, first_y if u == 0 else all_y)
                    sp.dma_start(out[b - 1, u * P:(u + 1) * P], y[:, u, :]).then_inc(y_stored, 16)
                sp.wait_ge(y_stored, stored)
                sp.sem_inc(y_free, 1)
            place_v(1, at(B - 2, U, 1), at(B - 1, U, 0), range(NQ // 2))
            place_k(0, at(B - 1, U, 0), at(B - 1, 2 * U, 2))
            place_k(1, at(B - 1, U, 1), at(B - 1, 2 * U, 4))
            place_v(0, at(B - 1, U, 0), at(B - 1, U, 1))
            place_v(1, at(B - 1, U, 1), at(B - 1, U, 2))
            for u in range(U):
                sp.wait_ge(y_made, at(B - 2, U, u + 1))
                sp.dma_start(out[B - 2, u * P:(u + 1) * P], y[:, u, :]).then_inc(y_stored, 16)
            sp.wait_ge(y_stored, at(B - 1, 16 * U, 0))
            sp.sem_inc(y_free, 1)
            sp.wait_ge(y_made, at(B - 1, U, 1))
            sp.dma_start(out[B - 1, 0:P], y[:, 0, :]).then_inc(last_stored, 16)
            sp.wait_ge(half_normalised, 1)
            sp.dma_start(out[B - 1, P:, HALVES[0]], y[:, 1, HALVES[0]]).then_inc(last_stored, 16)
            sp.wait_ge(last_stored, 3 * 16)

        @block.gpsimd
        def _(pool):
            def inverse_deviation(b, u, n):
                pool.wait_ge(moments_made[n], at(b, U, u + 1))
                nc.gpsimd.tensor_tensor(var_eps[:, n, u:u + 1], moments[:, n, u, 1:2], eps[:], ALU.add)\
                    .then_inc(eps_added[n], 1)
                pool.wait_ge(eps_added[n], at(b, U, u + 1))
                nc.gpsimd.tensor_tensor(rstd[:, n, u:u + 1], var_eps[:, n, u:u + 1], minus_half[:], ALU.pow)\
                    .then_inc(rstd_made[n], 1)

            def add_bias(b, u, w):
                pool.wait_ge(proj_kept, at(b, 3 * U, qk_place(b, u, w)))
                nc.gpsimd.tensor_tensor(qk_tok[:, w, u, 0:D], qk_tok[:, w, u, 0:D], bias[:, w, :], ALU.add)\
                    .then_inc(biased, 1)

            def add_bias_v(b, u):
                pool.wait_ge(proj_kept, at(b, 3 * U, 2 * U + u + 1))
                nc.gpsimd.tensor_tensor(v_tok[:, u, :], v_tok[:, u, :], bias[:, 2, :], ALU.add).then_inc(biased, 1)

            def step(b):
                add_bias(b, 0, 0)
                add_bias(b, 0, 1)
                add_bias(b, 1, 0)
                inverse_deviation(b - 1, 0, 0)
                add_bias(b, 1, 1)
                inverse_deviation(b - 1, 1, 0)
                add_bias_v(b, 0)
                add_bias_v(b, 1)

            pool.sem_inc(y_free, 1)
            nc.gpsimd.memset(ident[:], 0.0).then_inc(consts_set, 1)
            nc.gpsimd.memset(minus_half[:], -0.5).then_inc(consts_set, 1)
            nc.gpsimd.memset(eps[:], LN_EPS).then_inc(consts_set, 1)
            pool.wait_ge(consts_set, 3)
            nc.gpsimd.affine_select(out=ident[:], in_=ident[:], compare_op=ALU.not_equal, fill=1.0, base=0,
                                    pattern=[[-1, P]], channel_multiplier=1).then_inc(ident_ready, 1)
            nc.gpsimd.memset(qk_tok[:, :, :, D:], 0.0).then_inc(pads_ready, 1)
            nc.gpsimd.memset(k_diag[:], 0.0).then_inc(k_diag_zero, 1)
            for w in range(2):
                pool.wait_ge(bias_loaded[w], 16)
                for u in range(U):
                    add_bias(0, u, w)
            pool.wait_ge(w_turned, 3 * C)
            nc.gpsimd.memset(v_diag[:], 0.0).then_inc(v_diag_zero, 1)
            pool.wait_ge(bias_loaded[2], 16)
            for u in range(U):
                add_bias_v(0, u)
            with pool.Fori(1, B - 1) as b:
                step(b)
                for u in range(U):
                    inverse_deviation(b - 1, u, 1)
            step(B - 1)
            for u in range(U):
                inverse_deviation(B - 1, u, 0)
            for u in range(U):
                inverse_deviation(B - 2, u, 1)
            for u in range(U):
                inverse_deviation(B - 1, u, 1)

        @block.scalar
        def _(act):
            def weight_high(n):
                act.wait_ge(w_turned, n + 1)
                nc.scalar.copy(w_hi[:, n // C, n % C, :], weight_bank(n)).then_inc(w_hi_made, 1)

            def x_high(b, u, x1_done=None):
                act.wait_ge(x_turned, at(b, U, u + 1))
                if u and x1_done is not None:
                    act.wait_ge(x1_used, x1_done)
                nc.scalar.copy(feat_hi[:, :, u * P:(u + 1) * P],
                               ps_turn[:, u, :].rearrange("p (c t) -> p c t", c=C)).then_inc(x_hi_made, 1)

            def x_for_v(b, outputs_done=None):
                if outputs_done is not None:
                    act.wait_ge(out_made, outputs_done)
                for made, source, target in ((x_hi_made, feat_hi, xv_hi), (x_lo_made, feat_lo, xv_lo)):
                    for u in range(U):
                        act.wait_ge(made, at(b, U, u + 1))
                        nc.scalar.copy(target[:, u].rearrange("p c (k m) -> p c k m", k=NQ),
                                       source[:, :, u * P:(u + 1) * P].bitcast(F32)
                                       .rearrange("p c (m k) -> p c k m", k=NQ)).then_inc(xv_made, 1)

            def keep_x(b):
                wait_if_any(act, x1_made, at(b, U, 0))
                if isinstance(b, int) and b == 0:
                    act.wait_ge(x0_loaded, 16)
                act.wait_ge(x_loaded, at(b, 16, 16))
                nc.scalar.copy(pre1, x_in[:]).then_inc(x_kept, 1)

            def keep(b, u, w):
                place = qk_place(b, u, w)
                act.wait_ge(proj_made, at(b, 3 * U, place))
                nc.scalar.copy(qk_tok[:, w, u, 0:D], ps_lin[:, (place - 1) % 2, :]).then_inc(proj_kept, 1)

            def keep_qk(b, u):
                act.wait_ge(qk_turned, at(b - 1, 2 * U, 2 * u + 2))
                for w in range(2):
                    keep(b, u, w)

            def keep_v(b, u):
                wait_if_any(act, y_free, b)
                act.wait_ge(proj_made, at(b, 3 * U, 2 * U + u + 1))
                nc.scalar.copy(v_tok[:, u, :], ps_lin[:, u, :]).then_inc(proj_kept, 1)

            def x1_high(b):
                for c in range(C):
                    act.wait_ge(x1_turned, at(b, 2, c // 2 + 1))
                    nc.scalar.activation(feat_hi[:, c, :], ps_turn[:, c // 2, c % 2 * S:(c % 2 + 1) * S], ACT.Copy,
                                         accum_out=x1_sum[:, c:c + 1]).then_inc(x1_hi_made, 1)

            def gate_exp(b, bank=1):
                act.wait_ge(gbias_made, b + 1)
                nc.scalar.activation(gexp[:], ps_lin[:, bank, 0:E], ACT.Exp, bias=gbias[:], scale=GATE_SCALE,
                                     accum_out=gsum[:]).then_inc(gexp_made, 1)

            def exponentials(b, u):
                act.wait_ge(shifted, at(b, U, u + 1))
                nc.scalar.activation(probs[:, u], probs[:, u], ACT.Exp, scale=SCORE_SCALE).then_inc(exp_made, 1)

            def h_high(b, fill=None):
                act.wait_ge(coef_made, at(b, EPC, EPC))
                for m in range(M):
                    if m == M // 2 and fill:
                        fill()
                    act.wait_ge(h_made, at(b, M // 2, m // 2 + 1))
                    nc.scalar.mul(h_hi[:, m, :], ps_turn[:, m // 2, m % 2 * S:(m % 2 + 1) * S],
                                  coef[:, m:m + 1]).then_inc(h_hi_made, 1)

            def place_rest_of_v(b):
                act.wait_ge(v_turned, at(b, U, U))
                act.wait_ge(ctx_made, at(b, U, 1))
                for c in range(NQ // 2, NQ):
                    act.dma_start(v_diag[Q * c:Q * c + Q, c, 0:HD, :], v_T[Q * c:Q * c + Q, 1, :, :])\
                        .then_inc(v_placed, 16)

            def step(b):
                keep_qk(b, 0)
                place_rest_of_v(b - 1)
                keep_qk(b, 1)
                for u in range(U):
                    keep_v(b, u)
                keep_x(b)
                x1_high(b - 1)
                exponentials(b, 0)
                gate_exp(b - 1)
                h_high(b - 1, fill=lambda: exponentials(b, 1))

            def weights_high(*numbers):
                for n in numbers:
                    weight_high(n)

            x_high(0, 0)
            weights_high(0, 1, 2, 3)
            act.dma_start(w_raw[3], w_org.rearrange("(c p) i -> p c i", p=P)).then_inc(w_loaded[3], 16)
            x_high(0, 1)
            act.wait_ge(pads_ready, 1)
            keep(0, 0, 0)
            weights_high(4, 5)
            keep(0, 1, 0)
            weights_high(6, 7, 8)
            x_for_v(0)
            keep(0, 0, 1)
            weights_high(9, 10)
            keep(0, 1, 1)
            weights_high(11, 12, 13, 14, 15)
            keep_x(0)
            act.dma_start(up_raw, lora_up.rearrange("e r o -> (e r) o").rearrange("(m p) o -> p m o", p=P))\
                .then_inc(up_loaded, 16)
            act.wait_ge(down_loaded, 16 * C)
            nc.scalar.copy(down_hi[:], down_raw).then_inc(down_hi_made, 1)
            keep_v(0, 0)
            act.wait_ge(up_loaded, 16)
            nc.scalar.copy(up_hi[:], up_raw).then_inc(up_hi_made, 1)
            keep_v(0, 1)
            exponentials(0, 0)
            for u in range(U):
                x_high(1, u)
            x_for_v(1)
            exponentials(0, 1)
            with act.Fori(1, B - 1) as b:
                step(b)
                for u in range(U):
                    x_high(b + 1, u, x1_done=b)
                x_for_v(b + 1, outputs_done=at(b, U, 0))
            step(B - 1)
            x1_high(B - 1)
            gate_exp(B - 1, 0)
            h_high(B - 1)
            act.wait_ge(half_normalised, 2)
            act.dma_start(out[B - 1, P:, HALVES[1]], y[:, 1, HALVES[1]]).then_inc(last_stored, 16)

        @block.vector
        def _(dve):
            def weight_low(n):
                dve.wait_ge(w_hi_made, n + 1)
                nc.vector.tensor_tensor(w_lo[:, n // C, n % C, :], weight_bank(n),
                                        w_hi[:, n // C, n % C, :].bitcast(F32), ALU.subtract).then_inc(w_lo_made, 1)

            def weights_low(*numbers):
                for n in numbers:
                    weight_low(n)

            def x_low(b, u):
                dve.wait_ge(x_hi_made, at(b, U, u + 1))
                nc.vector.tensor_tensor(feat_lo[:, :, u * P:(u + 1) * P],
                                        ps_turn[:, u, :].rearrange("p (c t) -> p c t", c=C),
                                        feat_hi[:, :, u * P:(u + 1) * P].bitcast(F32),
                                        ALU.subtract).then_inc(x_lo_made, 1)

            def turn_heads(b, u, w):
                dve.wait_ge(biased, at(b, 3 * U, qk_place(b, u, w)))
                heads = qk_tok[:, w, u, :]
                squares = bass.AP(tensor=heads.tensor, offset=heads.offset, ap=[heads.ap[0], [HD, H], [1, Q]])
                nc.vector.transpose((q_T, k_T)[w][:, u].rearrange("p j h -> p h j"), squares).then_inc(qk_turned, 1)

            def turn_q(b, u):
                dve.wait_ge(scores_made, at(b - 1, U, u + 1))
                turn_heads(b, u, 0)

            def turn_k(b, u):
                dve.wait_ge(k_placed, at(b - 1, NQ * 16 * U, NQ * 16 * (u + 1)))
                turn_heads(b, u, 1)

            def turn_v(b, u, first=False):
                if not first:
                    dve.wait_ge(v_placed, at(b - 1, NQ * 16 * U, NQ * 16 * (u + 1)))
                dve.wait_ge(biased, at(b, 3 * U, 2 * U + u + 1))
                nc.vector.transpose(v_T[:, u], v_tok[:, u, :].rearrange("p (t d) -> p d t", d=HD))\
                    .then_inc(v_turned, 1)

            def shift_scores(b, u):
                scores = ps_att[:, u].rearrange("p a (m t) -> p (a m) t", t=H)
                dve.wait_ge(scores_made, at(b, U, u + 1))
                nc.vector.reduce_max(row_max[:, u, :], scores, AX_X).then_inc(max_made, 1)
                dve.wait_ge(max_made, at(b, U, u + 1))
                nc.vector.tensor_tensor(probs[:, u], scores, row_max[:, u, :].unsqueeze(2).to_broadcast([P, J, H]),
                                        ALU.subtract).then_inc(shifted, 1)

            def turn_probs(b, u):
                dve.wait_ge(exp_made, at(b, U, u + 1))
                nc.vector.transpose(probs_T[:, u], probs[:, u]).then_inc(probs_turned, 1)

            def moments_of(u, n, source):
                nc.vector.bn_stats(stats[:, n, u, :], source[:, u, :])
                dve.drain()
                nc.vector.bn_aggr(moments[:, n, u, :], stats[:, n, u, :]).then_inc(moments_made[n], 1)

            def normalise(b, u, n, target, source, made):
                dve.wait_ge(rstd_made[n], at(b, U, u + 1))
                nc.vector.tensor_scalar(target[:, u, :], source[:, u, :], moments[:, n, u, 0:1],
                                        rstd[:, n, u:u + 1], ALU.subtract, ALU.mult).then_inc(made, 1)

            def add_attention(b, u):
                dve.wait_ge(ctx_made, at(b, U, u + 1))
                source = ps_att[:, u, :, 0:HALF * NQ * DA].rearrange("p a (j d) -> p d a j", d=DA)
                nc.vector.transpose(ctx_tok[u], source).then_inc(ctx_turned, 1)
                dve.wait_ge(ctx_turned, at(b, U, u + 1))
                nc.vector.reciprocal(inv_sum[:, u, :], ctx_tok[u][:, HD, :]).then_inc(inv_made, 1)
                dve.wait_ge(inv_made, at(b, U, u + 1))
                nc.vector.tensor_tensor(ctx_tok[u][:, 0:HD, :], ctx_tok[u][:, 0:HD, :],
                                        inv_sum[:, u, :].unsqueeze(1).to_broadcast([P, HD, H]),
                                        ALU.mult).then_inc(attn_made, 1)
                dve.wait_ge(attn_made, at(b, U, u + 1))
                dve.wait_ge(x_kept, b + 1)
                by_feature = pre1[:, u, :].rearrange("p (h d) -> p d h", h=H)
                nc.vector.tensor_tensor(by_feature, by_feature, ctx_tok[u][:, 0:HD, :], ALU.add)\
                    .then_inc(pre1_made, 1)
                dve.wait_ge(pre1_made, at(b, U, u + 1))
                moments_of(u, 0, pre1)

            def x1_low(b):
                for k in range(C // 2):
                    dve.wait_ge(x1_hi_made, at(b, C, 2 * k + 2))
                    chunks = slice(2 * k, 2 * k + 2)
                    nc.vector.tensor_tensor(feat_lo[:, chunks, :], ps_turn[:, k, :].rearrange("p (c t) -> p c t", c=2),
                                            feat_hi[:, chunks, :].bitcast(F32), ALU.subtract).then_inc(x1_lo_made, 1)

            def gate_shift(b, bank=1):
                dve.wait_ge(gscore_made, b + 1)
                nc.vector.reduce_max(gmax[:], ps_lin[:, bank, 0:E], AX_X).then_inc(gmax_made, 1)
                dve.wait_ge(gmax_made, b + 1)
                nc.vector.tensor_scalar(gbias[:], gmax[:], -GATE_SCALE, None, ALU.mult).then_inc(gbias_made, 1)

            def gate_coefficients(b):
                dve.wait_ge(gexp_made, b + 1)
                nc.vector.reciprocal(ginv[:], gsum[:]).then_inc(ginv_made, 1)
                dve.wait_ge(ginv_made, b + 1)
                for e in range(EPC):
                    rows = slice(R * e, R * (e + 1))
                    nc.vector.tensor_scalar(coef[rows, :], gexp[rows, e:E:EPC], ginv[rows, :], None, ALU.mult)\
                        .then_inc(coef_made, 1)

            def h_low(b, half):
                for m in range(M // 2 * half, M // 2 * (half + 1)):
                    dve.wait_ge(h_hi_made, at(b, M, m // 2 * 2 + 2))
                    nc.vector.scalar_tensor_tensor(h_lo[:, m, :], ps_turn[:, m // 2, m % 2 * S:(m % 2 + 1) * S],
                                                   coef[:, m:m + 1], h_hi[:, m, :].bitcast(F32),
                                                   ALU.mult, ALU.subtract).then_inc(h_lo_made, 1)

            def up_low(half):
                part = slice(half * M // 2, (half + 1) * M // 2)
                nc.vector.tensor_tensor(up_lo[:, part, :], up_raw[:, part, :], up_hi[:, part, :].bitcast(F32),
                                        ALU.subtract).then_inc(up_lo_made, 1)

            def add_outputs(b, u, x1=x1):
                dve.wait_ge(out_made, at(b, U, u + 1))
                nc.vector.tensor_tensor(pre2[:, u, :], ps_lin[:, u, :], x1[:, u, :], ALU.add).then_inc(pre2_made, 1)
                dve.wait_ge(pre2_made, at(b, U, U + u + 1))
                moments_of(u, 1, pre2)

            def step(b, before_last_low=None):
                turn_q(b, 0)
                turn_k(b, 0)
                add_attention(b - 1, 0)
                turn_q(b, 1)
                normalise(b - 1, 0, 0, x1, pre1, x1_made)
                turn_k(b, 1)
                add_attention(b - 1, 1)
                normalise(b - 1, 1, 0, x1, pre1, x1_made)
                shift_scores(b, 0)
                turn_v(b, 0)
                x1_low(b - 1)
                turn_v(b, 1)
                turn_probs(b, 0)
                gate_shift(b - 1)
                gate_coefficients(b - 1)
                shift_scores(b, 1)
                h_low(b - 1, 0)
                turn_probs(b, 1)
                if before_last_low:
                    before_last_low()
                h_low(b - 1, 1)

            dve.sem_inc(pre2_made, U)
            x_low(0, 0)
            weights_low(0, 1, 2, 3)
            x_low(0, 1)
            weights_low(4, 5, 6, 7)
            turn_heads(0, 0, 0)
            weights_low(8)
            turn_heads(0, 1, 0)
            weights_low(9, 10)
            turn_heads(0, 0, 1)
            dve.wait_ge(keys_turned, 1)
            nc.vector.tensor_copy(keys_T[:], ps_turn[:, 0, 0:E]).then_inc(keys_kept, 1)
            weights_low(11, 12, 13, 14, 15)
            turn_heads(0, 1, 1)
            dve.wait_ge(down_hi_made, 1)
            nc.vector.tensor_tensor(down_lo[:], down_raw, down_hi[:].bitcast(F32), ALU.subtract)\
                .then_inc(down_lo_made, 1)
            dve.wait_ge(v_diag_zero, 1)
            for c in range(NQ):
                nc.vector.memset(v_diag[Q * c:Q * c + Q, c, HD, :], 1.0).then_inc(ones_placed, 1)
            turn_v(0, 0, first=True)
            dve.wait_ge(gate_made, 1)
            nc.vector.tensor_copy(gate[:], ps_turn[:, 1, 0:C * E].rearrange("p (c e) -> p c e", c=C))\
                .then_inc(gate_kept, 1)
            dve.wait_ge(down_lo_made, 1)
            shift_scores(0, 0)
            dve.wait_ge(up_hi_made, 1)
            up_low(0)
            for u in range(U):
                x_low(1, u)
            dve.wait_ge(up_lo_made, 1)
            turn_probs(0, 0)
            shift_scores(0, 1)
            turn_v(0, 1, first=True)
            up_low(1)
            dve.wait_ge(up_lo_made, 2)
            turn_probs(0, 1)
            with dve.Fori(1, B - 1) as b:
                step(b)
                add_outputs(b - 1, 0)
                x_low(b + 1, 0)
                normalise(b - 1, 0, 1, y, pre2, y_made)
                x_low(b + 1, 1)
                add_outputs(b - 1, 1)
                normalise(b - 1, 1, 1, y, pre2, y_made)
            step(B - 1, before_last_low=lambda: add_attention(B - 1, 0))
            add_attention(B - 1, 1)
            normalise(B - 1, 0, 0, pre1, pre1, x1_made)
            normalise(B - 1, 1, 0, pre1, pre1, x1_made)
            add_outputs(B - 2, 0)
            x1_low(B - 1)
            normalise(B - 2, 0, 1, y, pre2, y_made)
            add_outputs(B - 2, 1)
            normalise(B - 2, 1, 1, y, pre2, y_made)
            gate_shift(B - 1, 0)
            gate_coefficients(B - 1)
            for half in range(2):
                h_low(B - 1, half)
            dve.wait_ge(y_free, B)
            add_outputs(B - 1, 0, pre1)
            normalise(B - 1, 0, 1, y, pre2, y_made)
            for n, cols in enumerate(HALVES):
                dve.wait_ge(half_made, n + 1)
                nc.vector.tensor_tensor(pre2[:, 1, cols], half_banks[n], pre1[:, 1, cols], ALU.add)\
                    .then_inc(half_added, 1)
                dve.wait_ge(half_added, n + 1)
                nc.vector.bn_stats(stats[:, 1, n, :], pre2[:, 1, cols])
            dve.drain()
            nc.vector.bn_aggr(moments[:, 1, 1, :], stats[:, 1, :, :]).then_inc(moments_made[1], 1)
            dve.wait_ge(rstd_made[1], at(B - 1, U, 2))
            for cols in HALVES:
                nc.vector.tensor_scalar(y[:, 1, cols], pre2[:, 1, cols], moments[:, 1, 1, 0:1], rstd[:, 1, 1:2],
                                        ALU.subtract, ALU.mult).then_inc(half_normalised, 1)

        @block.tensor
        def _(pe):
            def product(out, left, right, first, last):
                nc.tensor.matmul(out, left[0], right[0], start=first, stop=False)
                nc.tensor.matmul(out, left[0], right[1], start=False, stop=False)
                return nc.tensor.matmul(out, left[1], right[0], start=False, stop=last)

            def turn_weight(w, *chunks):
                for c in chunks:
                    n = w * C + c
                    if w:
                        pe.wait_ge(w_loaded[w], 16)
                    else:
                        pe.wait_ge(wq_first_loaded if c < C // 2 else wq_rest_loaded, 16)
                    wait_if_any(pe, w_lo_made, n - 3)
                    for o in range(C):
                        ins = nc.tensor.transpose(weight_bank(n)[:, o * P:(o + 1) * P],
                                                  w_raw[w][:, o, c * P:(c + 1) * P], ident[:])
                    ins.then_inc(w_turned, 1)

            def turn_x_tile(u):
                for c in range(C):
                    ins = nc.tensor.transpose(ps_turn[:, u, c * P:(c + 1) * P], x_in[:, u, c * P:(c + 1) * P],
                                              ident[:])
                ins.then_inc(x_turned, 1)

            def turn_x(b):
                pe.wait_ge(x_loaded, at(b, 16, 16))
                for u in range(U):
                    turn_x_tile(u)

            def project_qk(b, u, w, before_chunk=None):
                pe.wait_ge(x_lo_made, at(b, U, u + 1))
                place = qk_place(b, u, w)
                bank = (place - 1) % 2
                if place > 2:
                    pe.wait_ge(proj_kept, at(b, 3 * U, place - 2))
                elif not isinstance(b, int) or b:
                    pe.wait_ge(pre2_made, at(b - 1, U, bank + 1))
                for c in range(C):
                    if before_chunk:
                        before_chunk(c)
                    cols = slice(u * P, (u + 1) * P)
                    ins = product(ps_lin[:, bank, :], (feat_hi[:, c, cols], feat_lo[:, c, cols]),
                                  (w_hi[:, w, c, :], w_lo[:, w, c, :]), c == 0, c == C - 1)
                ins.then_inc(proj_made, 1)

            def project_v(b, u, before_chunk=None):
                pe.wait_ge(xv_made, at(b, 2 * U, U + u + 1))
                pe.wait_ge(proj_kept, at(b, 3 * U, 2 * U + u - 1))
                for c in range(C):
                    if before_chunk:
                        before_chunk(c)
                    ins = product(ps_lin[:, u, :], (xv_hi[:, u, c, :], xv_lo[:, u, c, :]),
                                  (w_hi[:, 2, c, :], w_lo[:, 2, c, :]), c == 0, c == C - 1)
                ins.then_inc(proj_made, 1)

            def scores(b, u, first=False):
                if not first:
                    pe.wait_ge(ctx_turned, at(b - 1, U, u + 1))
                pe.wait_ge(k_placed, at(b, NQ * 16 * U, NQ * 16 * (u + 1)))
                for g in range(G):
                    for c in range(NQ):
                        j = NQ * g + c
                        cols = slice(g % HALF * P, (g % HALF + 1) * P)
                        ins = nc.tensor.matmul(ps_att[Q * c:Q * c + Q, u, g // HALF, cols]
                                               .rearrange("h (r t) -> h r t", r=NQ),
                                               q_T[:, u, j, :], k_diag[:, :, j, :], start=True, stop=True)
                ins.then_inc(scores_made, 1)

            def context(b, u):
                pe.wait_ge(v_placed, at(b, NQ * 16 * U, NQ * 16 * (u + 1)))
                pe.wait_ge(probs_turned, at(b, U, u + 1))
                for g in range(G):
                    for r in range(NQ):
                        cols = slice(g % HALF * NQ * DA, (g % HALF + 1) * NQ * DA)
                        ins = nc.tensor.matmul(ps_att[Q * r:Q * r + Q, u, g // HALF, cols]
                                               .rearrange("h (c d) -> h c d", c=NQ),
                                               probs_T[:, u, NQ * g + r, :], v_diag[:, :, :, G * r + g],
                                               start=True, stop=True)
                ins.then_inc(ctx_made, 1)

            def turn_x1(b, x1):
                pe.wait_ge(x1_made, at(b, U, U))
                for c in range(C):
                    for u in range(U):
                        place = c % 2 * S + u * P
                        ins = nc.tensor.transpose(ps_turn[:, c // 2, place:place + P], x1[:, u, c * P:(c + 1) * P],
                                                  ident[:])
                    if c % 2:
                        ins.then_inc(x1_turned, 1)

            def gate_scores(b, bank):
                pe.wait_ge(x1_hi_made, at(b, C, C))
                for r in range(NQ):
                    for c in range(C):
                        ins = nc.tensor.matmul(ps_lin[Q * r:Q * r + Q, bank, 0:E],
                                               x1_sum[:, c:c + 1].to_broadcast([P, Q]),
                                               gate[:, c, :], start=(c == 0), stop=(c == C - 1))
                ins.then_inc(gscore_made, 1)

            def hidden(b, between=None):
                pe.wait_ge(x1_lo_made, at(b, C // 2, C // 2))
                for m in range(M):
                    if m == M // 2 and between:
                        between()
                    rows = slice(m * P, (m + 1) * P)
                    for c in range(C):
                        ins = product(ps_turn[:, m // 2, m % 2 * S:(m % 2 + 1) * S],
                                      (down_hi[:, c, rows], down_lo[:, c, rows]), (feat_hi[:, c, :], feat_lo[:, c, :]),
                                      c == 0, c == C - 1)
                    if m % 2:
                        ins.then_inc(h_made, 1)

            def outputs(b, u, between=None):
                cols = slice(u * P, (u + 1) * P)
                for c in range(C):
                    ins = product(ps_lin[:, u, :], (feat_hi[:, c, cols], feat_lo[:, c, cols]),
                                  (w_hi[:, 3, c, :], w_lo[:, 3, c, :]), c == 0, False)
                if u:
                    ins.then_inc(x1_used, 1)
                if between:
                    between()
                for m in range(M):
                    if u == 0:
                        pe.wait_ge(h_lo_made, at(b, M, m + 1))
                    ins = product(ps_lin[:, u, :], (h_hi[:, m, cols], h_lo[:, m, cols]),
                                  (up_hi[:, m, :], up_lo[:, m, :]), False, m == M - 1)
                ins.then_inc(out_made, 1)

            def step(b, in_hidden=None):
                for w in range(2):
                    project_qk(b, 0, w)
                context(b - 1, 0)
                for w in range(2):
                    project_qk(b, 1, w)
                context(b - 1, 1)
                scores(b, 0)
                for u in range(U):
                    project_v(b, u)
                turn_x1(b - 1, x1)
                scores(b, 1)
                pe.wait_ge(proj_kept, at(b, 3 * U, 3 * U))
                gate_scores(b - 1, 1)
                hidden(b - 1, in_hidden)
                pe.wait_ge(gexp_made, b)

            pe.wait_ge(ident_ready, 1)
            pe.wait_ge(x0_loaded, 16)
            turn_x_tile(0)
            turn_weight(0, *range(C))
            pe.wait_ge(x_loaded, 16)
            turn_x_tile(1)
            project_qk(0, 0, 0, lambda c: pe.wait_ge(w_lo_made, c + 1))
            turn_weight(1, 0, 1)
            project_qk(0, 1, 0)
            turn_weight(1, 2, 3)
            turn_weight(2, 0)
            project_qk(0, 0, 1, lambda c: pe.wait_ge(w_lo_made, C + c + 1))
            pe.wait_ge(gate_loaded, 2 * 16)
            nc.tensor.transpose(ps_turn[:, 0, 0:E], keys[:], ident[0:E, 0:E]).then_inc(keys_turned, 1)
            turn_weight(2, 1, 2)
            project_qk(0, 1, 1)
            turn_weight(2, 3)
            turn_weight(3, *range(C))
            project_v(0, 0, lambda c: pe.wait_ge(w_lo_made, 2 * C + c + 1))
            pe.wait_ge(w_lo_made, 4 * C)
            scores(0, 0, first=True)
            pe.wait_ge(keys_kept, 1)
            for c in range(C):
                ins = nc.tensor.matmul(ps_turn[:, 1, c * E:(c + 1) * E], gate_raw[:, c * P:(c + 1) * P], keys_T[:],
                                       start=True, stop=True)
            ins.then_inc(gate_made, 1)
            project_v(0, 1)
            pe.wait_ge(gate_kept, 1)
            turn_x(1)
            scores(0, 1, first=True)
            pe.wait_ge(ones_placed, NQ)
            with pe.Fori(1, B - 1) as b:
                step(b)
                outputs(b - 1, 0)
                turn_x(b + 1)
                outputs(b - 1, 1)
            step(B - 1, in_hidden=lambda: context(B - 1, 0))
            outputs(B - 2, 0, between=lambda: context(B - 1, 1))
            outputs(B - 2, 1, between=lambda: turn_x1(B - 1, pre1))
            pe.wait_ge(pre2_made, at(B - 1, U, 1))
            gate_scores(B - 1, 0)
            hidden(B - 1)
            pe.wait_ge(gexp_made, B)
            outputs(B - 1, 0)
            pe.wait_ge(pre2_made, at(B - 1, U, 2))
            for n, cols in enumerate(HALVES):
                for c in range(C):
                    product(half_banks[n], (feat_hi[:, c, P:], feat_lo[:, c, P:]),
                            (w_hi[:, 3, c, cols], w_lo[:, 3, c, cols]), c == 0, False)
                for m in range(M):
                    ins = product(half_banks[n], (h_hi[:, m, P:], h_lo[:, m, P:]),
                                  (up_hi[:, m, cols], up_lo[:, m, cols]), False, m == M - 1)
                ins.then_inc(half_made, 1)


_INS = ['L0_attn_hidden_states', 'L0_attn_wq', 'L0_attn_bq', 'L0_attn_wk', 'L0_attn_bk', 'L0_attn_wv', 'L0_attn_bv',
        'L0_ffn_W_org', 'L0_ffn_lora_down', 'L0_ffn_lora_up', 'L0_ffn_lora_keys', 'L0_ffn_Wq']


def kernel(**inputs):
    import numpy as _np
    import concourse.bacc as _bacc
    from concourse import mybir as _mybir
    from concourse.bass_utils import run_bass_kernel_spmd as _run

    nc = _bacc.Bacc("TRN2", target_bir_lowering=False, num_devices=1)
    arrays, args = {}, []
    for name in _INS:
        a = _np.ascontiguousarray(inputs[name])
        arrays[f"in_{name}_dram"] = a
        args.append(nc.dram_tensor(f"in_{name}_dram", a.shape, _mybir.dt.from_np(a.dtype), kind="ExternalInput").ap())
    shape = inputs['L0_attn_hidden_states'].shape
    args.append(nc.dram_tensor("out_0_dram", shape, _mybir.dt.float32, kind="ExternalOutput").ap())
    seq_postln_kernel(nc, *args)
    r = _run(nc, [arrays], core_ids=[0])
    return r.results[0]["out_0_dram"]
```
